# Optimizing a Trainium2 kernel written in Bass

```python
import numpy as np
import jax
import jax.numpy as jnp

def _softmax(x, axis=-1):
    return jax.nn.softmax(x, axis=axis)

def _gelu(x):
    return jax.nn.gelu(x, approximate=True)

def _silu(x):
    return jax.nn.silu(x)

def _sigmoid(x):
    return jax.nn.sigmoid(x)

def _layernorm(x, axis=-1, eps=1e-05):
    m = jnp.mean(x, axis=axis, keepdims=True)
    v = jnp.var(x, axis=axis, keepdims=True)
    return (x - m) / jnp.sqrt(v + eps)

def _scatter_add(tgt, idx, src, axis=0):
    return tgt.at[idx].add(src)

def _segment_sum(src, seg, n):
    return jax.ops.segment_sum(src, seg, n)
kernel_name = 'mk_rec_standalone_d1_rec_r8_d56f49'

def setup_inputs(seed: int=0):
    np.random.seed(seed)
    _w = jnp.asarray

    def _rec_inputs():
        import jax
        import jax.numpy as jnp
        _rk = jax.random.key(seed)
        r_feature_vals = jax.random.uniform(jax.random.fold_in(_rk, 1), (1024, 39), jnp.float32, 0.0, 0.999994)
        r_feature_ids = jnp.stack([jax.random.randint(jax.random.fold_in(jax.random.fold_in(_rk, 2), 0), (1024,), 331, 999050, jnp.int32), jax.random.randint(jax.random.fold_in(jax.random.fold_in(_rk, 2), 1), (1024,), 18, 999393, jnp.int32), jax.random.randint(jax.random.fold_in(jax.random.fold_in(_rk, 2), 2), (1024,), 148, 999903, jnp.int32), jax.random.randint(jax.random.fold_in(jax.random.fold_in(_rk, 2), 3), (1024,), 200, 999114, jnp.int32), jax.random.randint(jax.random.fold_in(jax.random.fold_in(_rk, 2), 4), (1024,), 1, 999794, jnp.int32), jax.random.randint(jax.random.fold_in(jax.random.fold_in(_rk, 2), 5), (1024,), 1565, 999412, jnp.int32), jax.random.randint(jax.random.fold_in(jax.random.fold_in(_rk, 2), 6), (1024,), 6, 998490, jnp.int32), jax.random.randint(jax.random.fold_in(jax.random.fold_in(_rk, 2), 7), (1024,), 200, 999767, jnp.int32), jax.random.randint(jax.random.fold_in(jax.random.fold_in(_rk, 2), 8), (1024,), 81, 999567, jnp.int32), jax.random.randint(jax.random.fold_in(jax.random.fold_in(_rk, 2), 9), (1024,), 341, 999667, jnp.int32), jax.random.randint(jax.random.fold_in(jax.random.fold_in(_rk, 2), 10), (1024,), 145, 999142, jnp.int32), jax.random.randint(jax.random.fold_in(jax.random.fold_in(_rk, 2), 11), (1024,), 1013, 999756, jnp.int32), jax.random.randint(jax.random.fold_in(jax.random.fold_in(_rk, 2), 12), (1024,), 1554, 999549, jnp.int32), jax.random.randint(jax.random.fold_in(jax.random.fold_in(_rk, 2), 13), (1024,), 725, 999945, jnp.int32), jax.random.randint(jax.random.fold_in(jax.random.fold_in(_rk, 2), 14), (1024,), 3, 997894, jnp.int32), jax.random.randint(jax.random.fold_in(jax.random.fold_in(_rk, 2), 15), (1024,), 62, 999267, jnp.int32), jax.random.randint(jax.random.fold_in(jax.random.fold_in(_rk, 2), 16), (1024,), 71, 999716, jnp.int32), jax.random.randint(jax.random.fold_in(jax.random.fold_in(_rk, 2), 17), (1024,), 441, 999883, jnp.int32), jax.random.randint(jax.random.fold_in(jax.random.fold_in(_rk, 2), 18), (1024,), 1656, 999449, jnp.int32), jax.random.randint(jax.random.fold_in(jax.random.fold_in(_rk, 2), 19), (1024,), 564, 999303, jnp.int32), jax.random.randint(jax.random.fold_in(jax.random.fold_in(_rk, 2), 20), (1024,), 49, 999715, jnp.int32), jax.random.randint(jax.random.fold_in(jax.random.fold_in(_rk, 2), 21), (1024,), 158, 124841, jnp.int32), jax.random.randint(jax.random.fold_in(jax.random.fold_in(_rk, 2), 22), (1024,), 11, 999726, jnp.int32), jax.random.randint(jax.random.fold_in(jax.random.fold_in(_rk, 2), 23), (1024,), 1073, 999500, jnp.int32), jax.random.randint(jax.random.fold_in(jax.random.fold_in(_rk, 2), 24), (1024,), 29, 999811, jnp.int32), jax.random.randint(jax.random.fold_in(jax.random.fold_in(_rk, 2), 25), (1024,), 150, 124982, jnp.int32), jax.random.randint(jax.random.fold_in(jax.random.fold_in(_rk, 2), 26), (1024,), 770, 999483, jnp.int32), jax.random.randint(jax.random.fold_in(jax.random.fold_in(_rk, 2), 27), (1024,), 131, 999906, jnp.int32), jax.random.randint(jax.random.fold_in(jax.random.fold_in(_rk, 2), 28), (1024,), 1371, 998078, jnp.int32), jax.random.randint(jax.random.fold_in(jax.random.fold_in(_rk, 2), 29), (1024,), 433, 998972, jnp.int32), jax.random.randint(jax.random.fold_in(jax.random.fold_in(_rk, 2), 30), (1024,), 39, 124968, jnp.int32), jax.random.randint(jax.random.fold_in(jax.random.fold_in(_rk, 2), 31), (1024,), 275, 999919, jnp.int32), jax.random.randint(jax.random.fold_in(jax.random.fold_in(_rk, 2), 32), (1024,), 137, 999409, jnp.int32), jax.random.randint(jax.random.fold_in(jax.random.fold_in(_rk, 2), 33), (1024,), 171, 999404, jnp.int32), jax.random.randint(jax.random.fold_in(jax.random.fold_in(_rk, 2), 34), (1024,), 363, 999419, jnp.int32), jax.random.randint(jax.random.fold_in(jax.random.fold_in(_rk, 2), 35), (1024,), 136, 999338, jnp.int32), jax.random.randint(jax.random.fold_in(jax.random.fold_in(_rk, 2), 36), (1024,), 276, 999885, jnp.int32), jax.random.randint(jax.random.fold_in(jax.random.fold_in(_rk, 2), 37), (1024,), 444, 999830, jnp.int32), jax.random.randint(jax.random.fold_in(jax.random.fold_in(_rk, 2), 38), (1024,), 42, 999317, jnp.int32)], axis=1)
        return (r_feature_vals, r_feature_ids)
    r_feature_vals, r_feature_ids = _rec_inputs()

    def _L0_rec_setup():
        import jax, jax.numpy as jnp
        import numpy as np
        NUM_FEATURES = 125000
        EMB_DIM = 16
        NUM_FIELDS = 39
        CIN_SIZES = (200, 200, 200)
        DNN_SIZES = (400, 400)

        def _forward(feature_ids, feature_vals, emb, bias_emb, cin_W0, cin_b0, cin_W1, cin_b1, cin_W2, cin_b2, dnn_W0, dnn_b0, dnn_W1, dnn_b1, fc_W, fc_b):
            B = feature_ids.shape[0]
            inputs = emb[feature_ids] * feature_vals[:, :, None]
            input_biases = bias_emb[feature_ids][..., 0] * feature_vals
            Ws = (cin_W0, cin_W1, cin_W2)
            bs = (cin_b0, cin_b1, cin_b2)
            h = inputs
            finals = []
            n_layers = len(CIN_SIZES)
            for i in range(n_layers):
                size = CIN_SIZES[i]
                x = jnp.einsum('bhd,bmd->bhmd', h, inputs)
                x = x.reshape(B, -1, EMB_DIM)
                x = jnp.einsum('bcd,oc->bod', x, Ws[i]) + bs[i][None, :, None]
                x = jax.nn.relu(x)
                if i != n_layers - 1:
                    h, direct = (x[:, :size // 2], x[:, size // 2:])
                else:
                    direct = x
                finals.append(direct)
            cin_result = jnp.sum(jnp.concatenate(finals, axis=1), axis=-1)
            d = inputs.reshape(B, -1)
            d = jax.nn.relu(d @ dnn_W0.T + dnn_b0)
            d = jax.nn.relu(d @ dnn_W1.T + dnn_b1)
            out = (jnp.concatenate((cin_result, d), axis=1) @ fc_W.T + fc_b)[:, 0]
            return out + jnp.sum(input_biases, axis=1)
        key = jax.random.key(seed)
        ks = jax.random.split(key, 16)
        B = 256
        inp = {}
        inp['feature_ids'] = jax.random.randint(ks[0], (B, NUM_FIELDS), 0, NUM_FEATURES)
        inp['feature_vals'] = jax.random.uniform(ks[1], (B, NUM_FIELDS), dtype=jnp.float32)
        inp['emb'] = jax.random.normal(ks[2], (NUM_FEATURES, EMB_DIM), jnp.float32) * 0.02
        inp['bias_emb'] = jax.random.normal(ks[3], (NUM_FEATURES, 1), jnp.float32) * 0.02
        field_nums = [NUM_FIELDS]
        for i, size in enumerate(CIN_SIZES):
            cin_in = field_nums[-1] * NUM_FIELDS
            inp[f'cin_W{i}'] = jax.random.normal(ks[4 + i], (size, cin_in), jnp.float32) / np.sqrt(cin_in)
            inp[f'cin_b{i}'] = jnp.zeros((size,), jnp.float32)
            field_nums.append(size // 2 if i != len(CIN_SIZES) - 1 else size)
        last = NUM_FIELDS * EMB_DIM
        for i, size in enumerate(DNN_SIZES):
            inp[f'dnn_W{i}'] = jax.random.normal(ks[8 + i], (size, last), jnp.float32) / np.sqrt(last)
            inp[f'dnn_b{i}'] = jnp.zeros((size,), jnp.float32)
            last = size
        hidden_size = sum(CIN_SIZES[:-1]) // 2 + CIN_SIZES[-1]
        fc_in = hidden_size + DNN_SIZES[-1]
        inp['fc_W'] = jax.random.normal(ks[12], (1, fc_in), jnp.float32) / np.sqrt(fc_in)
        inp['fc_b'] = jnp.zeros((1,), jnp.float32)
        return inp
    _L0_rec_all = _L0_rec_setup()
    _L0_rec_in = {k: v for k, v in _L0_rec_all.items() if k in ('emb', 'bias_emb', 'cin_W0', 'cin_b0', 'cin_W1', 'cin_b1', 'cin_W2', 'cin_b2', 'dnn_W0', 'dnn_b0', 'dnn_W1', 'dnn_b1', 'fc_W', 'fc_b')}
    del _L0_rec_all
    return {'r_feature_vals': r_feature_vals, 'r_feature_ids': r_feature_ids, 'L0_rec_emb': _L0_rec_in['emb'], 'L0_rec_bias_emb': _L0_rec_in['bias_emb'], 'L0_rec_cin_W0': _L0_rec_in['cin_W0'], 'L0_rec_cin_b0': _L0_rec_in['cin_b0'], 'L0_rec_cin_W1': _L0_rec_in['cin_W1'], 'L0_rec_cin_b1': _L0_rec_in['cin_b1'], 'L0_rec_cin_W2': _L0_rec_in['cin_W2'], 'L0_rec_cin_b2': _L0_rec_in['cin_b2'], 'L0_rec_dnn_W0': _L0_rec_in['dnn_W0'], 'L0_rec_dnn_b0': _L0_rec_in['dnn_b0'], 'L0_rec_dnn_W1': _L0_rec_in['dnn_W1'], 'L0_rec_dnn_b1': _L0_rec_in['dnn_b1'], 'L0_rec_fc_W': _L0_rec_in['fc_W'], 'L0_rec_fc_b': _L0_rec_in['fc_b']}

def reference(r_feature_vals, r_feature_ids, L0_rec_emb, L0_rec_bias_emb, L0_rec_cin_W0, L0_rec_cin_b0, L0_rec_cin_W1, L0_rec_cin_b1, L0_rec_cin_W2, L0_rec_cin_b2, L0_rec_dnn_W0, L0_rec_dnn_b0, L0_rec_dnn_W1, L0_rec_dnn_b1, L0_rec_fc_W, L0_rec_fc_b):
    import jax
    import jax.numpy as jnp

    def _L0_rec_ref(feature_ids, feature_vals, emb, bias_emb, cin_W0, cin_b0, cin_W1, cin_b1, cin_W2, cin_b2, dnn_W0, dnn_b0, dnn_W1, dnn_b1, fc_W, fc_b):
        import jax, jax.numpy as jnp
        import numpy as np
        NUM_FEATURES = 125000
        EMB_DIM = 16
        NUM_FIELDS = 39
        CIN_SIZES = (200, 200, 200)
        DNN_SIZES = (400, 400)

        def _forward(feature_ids, feature_vals, emb, bias_emb, cin_W0, cin_b0, cin_W1, cin_b1, cin_W2, cin_b2, dnn_W0, dnn_b0, dnn_W1, dnn_b1, fc_W, fc_b):
            B = feature_ids.shape[0]
            inputs = emb[feature_ids] * feature_vals[:, :, None]
            input_biases = bias_emb[feature_ids][..., 0] * feature_vals
            Ws = (cin_W0, cin_W1, cin_W2)
            bs = (cin_b0, cin_b1, cin_b2)
            h = inputs
            finals = []
            n_layers = len(CIN_SIZES)
            for i in range(n_layers):
                size = CIN_SIZES[i]
                x = jnp.einsum('bhd,bmd->bhmd', h, inputs)
                x = x.reshape(B, -1, EMB_DIM)
                x = jnp.einsum('bcd,oc->bod', x, Ws[i]) + bs[i][None, :, None]
                x = jax.nn.relu(x)
                if i != n_layers - 1:
                    h, direct = (x[:, :size // 2], x[:, size // 2:])
                else:
                    direct = x
                finals.append(direct)
            cin_result = jnp.sum(jnp.concatenate(finals, axis=1), axis=-1)
            d = inputs.reshape(B, -1)
            d = jax.nn.relu(d @ dnn_W0.T + dnn_b0)
            d = jax.nn.relu(d @ dnn_W1.T + dnn_b1)
            out = (jnp.concatenate((cin_result, d), axis=1) @ fc_W.T + fc_b)[:, 0]
            return out + jnp.sum(input_biases, axis=1)
        return _forward(feature_ids, feature_vals, emb, bias_emb, cin_W0, cin_b0, cin_W1, cin_b1, cin_W2, cin_b2, dnn_W0, dnn_b0, dnn_W1, dnn_b1, fc_W, fc_b)
    y = _L0_rec_ref(r_feature_ids, r_feature_vals, L0_rec_emb, L0_rec_bias_emb, L0_rec_cin_W0, L0_rec_cin_b0, L0_rec_cin_W1, L0_rec_cin_b1, L0_rec_cin_W2, L0_rec_cin_b2, L0_rec_dnn_W0, L0_rec_dnn_b0, L0_rec_dnn_W1, L0_rec_dnn_b1, L0_rec_fc_W, L0_rec_fc_b)
    return y

_drawn_inputs = setup_inputs


def setup_inputs(seed=0):
    import zlib

    import numpy as np

    out = dict(_drawn_inputs(seed))
    spreads = {'L0_rec_cin_b0': (0.0, 0.611),
     'L0_rec_cin_b1': (0.0, 0.8),
     'L0_rec_cin_b2': (0.0, 0.8),
     'L0_rec_dnn_b0': (0.0, 2.0),
     'L0_rec_dnn_b1': (0.0, 2.0)}
    factors = {'r_feature_vals': 3.775,
     'L0_rec_emb': 8.0,
     'L0_rec_bias_emb': 27.976,
     'L0_rec_cin_W0': 8.0,
     'L0_rec_cin_W1': 8.0,
     'L0_rec_cin_W2': 8.0,
     'L0_rec_dnn_W0': 8.0,
     'L0_rec_dnn_W1': 8.0}
    for name, (base, spread) in spreads.items():
        noise = np.random.default_rng([zlib.crc32(name.encode()), seed]).standard_normal(out[name].shape)
        drawn = base * np.exp(spread * noise) if base else spread * noise
        out[name] = jnp.asarray(drawn.astype(out[name].dtype))
    for name, factor in factors.items():
        out[name] = (out[name] * factor).astype(out[name].dtype)
    return out
```

```python
from contextlib import ExitStack

import concourse.bass as bass
from concourse import mybir

P = 128
BATCH = 1024
FIELDS = 39
DIM = 16
VOCAB = 125000
EMB_COLS = DIM + 1
OUTS = 200
HID = 100
DNN = 400
TILES = BATCH // P
CHUNKS = TILES * DIM

SHIFTS = FIELDS // 2 + 1
PAIRS = SHIFTS * FIELDS
X_ROW = FIELDS + SHIFTS - 1
K_LAYER = [PAIRS, HID * FIELDS, HID * FIELDS]
KT = [-(-(k + 1) // P) for k in K_LAYER]
KT0 = [0, KT[0], KT[0] + KT[1]]
KT_ALL = sum(KT)
COL0 = [P * k for k in KT0]
GROUP = 4
GROUPS = [-(-k // GROUP) for k in KT]
RING = 3
PIECES = [1, 4, 4]
HSPLIT = [-(-(2 * GROUP * P * j) // FIELDS) for j in range(4)] + [HID]

DENSE_K = [FIELDS * DIM, DNN]
ROWS = [[P] * k for k in KT] + [[min(P, k - t) for t in range(0, k, P)] for k in DENSE_K]
GROUPS += [-(-len(ROWS[job]) // GROUP) for job in (3, 4)]
FIRST, SECOND = 3, 4
DKT = len(ROWS[FIRST]) + len(ROWS[SECOND])

STAGE = 1000
STAGES = 8

F32 = mybir.dt.float32
F32R = mybir.dt.float32r
I32 = mybir.dt.int32
ALU = mybir.AluOpType
ACT = mybir.ActivationFunctionType
AX_X = mybir.AxisListType.X

PRO = GROUPS[0]
STEP = sum(GROUPS[0:3])
LAST = CHUNKS - 1
DENSE_STEP = GROUPS[FIRST] + GROUPS[SECOND]
CIN_GROUPS = STEP * CHUNKS


def first_group(i):
    return PRO + GROUPS[1] + GROUPS[0] + STEP * (i - 1)


def dense_group(i):
    return CIN_GROUPS + GROUPS[FIRST] + DENSE_STEP * (i - 1)


def groups_of(job, c):
    return [(job, c, q) for q in range(GROUPS[job])]


def step_groups(i):
    return groups_of(1, i) + groups_of(0, i + 1) + groups_of(2, i - 1)


def dense_groups(i):
    return groups_of(FIRST, i) + groups_of(SECOND, i - 1)


def group_tiles(job, q):
    return range(GROUP * q, min(GROUP * q + GROUP, len(ROWS[job])))


def group_parts(job, q):
    parts = []
    for t in group_tiles(job, q):
        at = (t % GROUP) * P
        if parts and parts[-1][0] == ROWS[job][t]:
            parts[-1] = (parts[-1][0], slice(parts[-1][1].start, at + P))
        else:
            parts.append((ROWS[job][t], slice(at, at + P)))
    return parts


def is_first(c):
    return isinstance(c, int) and c == 0


def tail_groups():
    return groups_of(1, LAST) + groups_of(2, LAST - 1) + groups_of(2, LAST) + groups_of(FIRST, 0) + dense_groups(1)


def rec_kernel(nc, vals, ids, table, w0_ab, w0_ba, w1, w2, d0, d0_b, d1, d1_b, fc_w, fc_b, out):
    with ExitStack() as ctx:
        def sb(name, shape, dt):
            return ctx.enter_context(nc.sbuf_tensor(name, shape, dt))

        def sem(name):
            return ctx.enter_context(nc.semaphore(name))

        W = sb("W", [P, KT_ALL * 2 * OUTS], F32R)
        prods = sb("prods", [P, KT_ALL * P], F32)
        xhi = sb("xhi", [P, RING, GROUP * P], F32R)
        xlo = sb("xlo", [P, RING, GROUP * P], F32R)
        xin = sb("xin", [P, CHUNKS * X_ROW], F32)
        raw = sb("raw", [P, FIELDS * EMB_COLS], F32)
        val = sb("val", [P, TILES * FIELDS], F32)
        idi = sb("idi", [P, TILES * FIELDS], I32)
        idf = sb("idf", [P, TILES * FIELDS], F32)
        neg = sb("neg", [P, TILES * FIELDS], F32)
        idx = sb("idx", [P, FIELDS], I32)
        fbias = sb("fbias", [P, TILES * FIELDS], F32)
        ident = sb("ident", [P, P], F32)
        fcw = sb("fcw", [P, 2 * OUTS + DNN], F32)
        fcb = sb("fcb", [P, 1], F32)
        acc_lo = sb("acc_lo", [P, 3, OUTS], F32)
        acc_sum = sb("acc_sum", [P, 3, OUTS], F32)
        h = [sb("h1", [P, HID], F32), sb("h2", [P, HID], F32)]
        spent = sb("spent", [P, 3, OUTS], F32)
        part = sb("part", [P, 3 * CHUNKS], F32)
        dense_part = sb("dense_part", [P, TILES], F32)
        sums = sb("sums", [P, 4 * TILES], F32)
        total = sb("total", [P, 3 * TILES], F32)
        score = sb("score", [P, TILES], F32)

        n0, n1 = len(ROWS[FIRST]) * DNN, len(ROWS[SECOND]) * DNN
        raw_d0 = prods[:, 0:n0].rearrange("p (k o) -> p k o", o=DNN)
        raw_d1 = prods[:, n0:n0 + n1].rearrange("p (k o) -> p k o", o=DNN)
        dense_bias = prods[:, n0 + n1:n0 + n1 + 2 * DNN]
        dense_w = W[:, 0:DKT * 2 * DNN].rearrange("p (k two o) -> p k two o", two=2, o=DNN)
        assert n0 + n1 + 2 * DNN <= COL0[2] and DKT * 2 * DNN <= KT0[2] * 2 * OUTS
        dense_x = raw[:, 0:DENSE_K[0]]
        at = COL0[2]
        dense_sum = [prods[:, at:at + DNN], prods[:, at + DNN:at + 2 * DNN]]
        dense_h = prods[:, at + 2 * DNN:at + 3 * DNN]
        dense_spent = prods[:, at + 3 * DNN:at + 4 * DNN]

        turn = [ctx.enter_context(nc.psum_tensor(f"turn{r}", [P, GROUP * P], F32)) for r in range(RING)]
        acc = [ctx.enter_context(nc.psum_tensor(f"acc{n}", [P, 512], F32)) for n in range(3)]

        s_small = sem("small_loaded")
        s_fc = sem("fc_loaded")
        s_stage = [sem(f"staged{n}") for n in range(STAGES)]
        s_wsum = sem("w0_summed")
        s_whi = sem("weights_high")
        s_wlo = sem("weights_low")
        s_pad = sem("pads_set")
        s_ident = sem("ident_set")
        s_ids = sem("ids_step")
        s_mark = sem("pool_waited")
        s_idx = sem("idx_copied")
        s_gather = sem("rows_gathered")
        s_xin = sem("inputs_scaled")
        s_prod = [sem(f"products{n}") for n in range(3)]
        s_turn = [sem(f"turned{n}") for n in range(5)]
        s_xhi = sem("x_high")
        s_xlo = sem("x_low")
        s_mm = sem("group_multiplied")
        s_acclo = [sem(f"acc_low_copied{n}") for n in range(3)]
        s_acc = [sem(f"acc_summed{n}") for n in range(5)]
        s_h = [sem("h1_ready"), sem("h2_ready")]
        s_dot = [sem(f"fc_dotted{n}") for n in range(3)]
        s_draw = sem("dense_raw_loaded")
        s_dwhi = sem("dense_weights_high")
        s_dwlo = sem("dense_weights_low")
        s_dx = sem("dense_x_copied")
        s_dh = sem("dense_hidden")
        s_ddot = sem("dense_dotted")
        s_fin = sem("final_step")
        s_out = sem("output_stored")

        block = ctx.enter_context(nc.Block())

        per = STAGE // OUTS
        pieces = []
        for layer, src in ((0, w0_ab), (1, w1), (2, w2)):
            for t in range(0, KT[layer], per):
                n = min(per, KT[layer] - t)
                pieces.append((src, t, KT0[layer] + t, n, "first" if layer == 0 else "whole"))
                if layer == 0:
                    pieces.append((w0_ba, t, KT0[layer] + t, n, "second"))
        splits = [i for i, p in enumerate(pieces) if p[4] != "first"]

        def staged(i):
            return prods[:, STAGE * (i % STAGES):STAGE * (i % STAGES) + pieces[i][3] * OUTS]

        def splits_before_reuse(i):
            old = i - STAGES + (pieces[i - STAGES][4] == "first")
            return sum(1 for k in splits if k <= old)

        def split_source(i):
            return staged(i - 1 if pieces[i][4] == "second" else i).rearrange("p (k o) -> p k o", o=OUTS)

        def weight_half(i, half):
            _, _, k0, n, _ = pieces[i]
            return W[:, k0 * 2 * OUTS:(k0 + n) * 2 * OUTS].rearrange(
                "p (k two o) -> p k two o", two=2, o=OUTS)[:, :, half, :]

        @block.sync
        def _(sp):
            sp.dma_start(idi[:], ids.rearrange("(p t) m -> p (t m)", p=P)).then_inc(s_small, 16)
            sp.dma_start(val[:], vals.rearrange("(p t) m -> p (t m)", p=P)).then_inc(s_small, 16)
            for i, (src, t, k0, n, kind) in enumerate(pieces):
                if i >= STAGES:
                    sp.wait_ge(s_wlo, splits_before_reuse(i))
                sp.dma_start(staged(i).rearrange("p (k o) -> p k o", k=n),
                             src[:, t:t + n, :]).then_inc(s_stage[i % STAGES], 16)
            sp.dma_start(fcw[:], fc_w.partition_broadcast(P)).then_inc(s_fc, 16)
            sp.dma_start(fcb[:], fc_b.partition_broadcast(P)).then_inc(s_fc, 16)
            sp.wait_ge(s_turn[0], GROUPS[0] * CHUNKS)
            sp.wait_ge(s_turn[1], GROUPS[1] * CHUNKS)
            sp.dma_start(raw_d0, d0).then_inc(s_draw, 16)
            sp.dma_start(raw_d1, d1).then_inc(s_draw, 16)
            sp.dma_start(dense_bias[:, 0:DNN], d0_b.partition_broadcast(P)).then_inc(s_draw, 16)
            sp.dma_start(dense_bias[:, DNN:2 * DNN], d1_b.partition_broadcast(P)).then_inc(s_draw, 16)
            sp.wait_ge(s_fin, 6)
            sp.dma_start(out.rearrange("(p t) -> p t", p=P), score[:]).then_inc(s_out, 16)
            sp.wait_ge(s_out, 16)

        @block.gpsimd
        def _(pool):
            def waited():
                pool.sem_inc(s_mark, 1)

            def copy_idx(tile):
                nc.gpsimd.tensor_copy(idx[:], idi[:, bass.ds(tile * FIELDS, FIELDS)]).then_inc(s_idx, 1)
                pool.wait_ge(s_idx, tile + 1)
                waited()

            def gather(m):
                nc.gpsimd.indirect_dma_start(
                    out=raw[:, m * EMB_COLS:(m + 1) * EMB_COLS], out_offset=None, in_=table,
                    in_offset=bass.IndirectOffsetOnAxis(ap=idx[:, m:m + 1], axis=0)).then_inc(s_gather, 16)

            def scale(tile):
                pool.wait_ge(s_gather, tile * (16 * FIELDS) + 16 * FIELDS)
                waited()
                rows = raw[:].rearrange("p (m d) -> p d m", d=EMB_COLS)
                v = val[:, bass.ds(tile * FIELDS, FIELDS)]
                x = xin[:, bass.ds(tile * (DIM * X_ROW), DIM * X_ROW)].rearrange("p (d x) -> p d x", x=X_ROW)
                more = X_ROW - FIELDS
                nc.gpsimd.tensor_tensor(x[:, :, 0:FIELDS], rows[:, 0:DIM, :],
                                        v.unsqueeze(1).broadcast_to([P, DIM, FIELDS]), ALU.mult).then_inc(s_xin, 1)
                nc.gpsimd.tensor_tensor(x[:, :, FIELDS:X_ROW], rows[:, 0:DIM, 0:more],
                                        v[:, 0:more].unsqueeze(1).broadcast_to([P, DIM, more]),
                                        ALU.mult).then_inc(s_xin, 1)
                nc.gpsimd.tensor_tensor(fbias[:, bass.ds(tile * FIELDS, FIELDS)], rows[:, DIM, :], v,
                                        ALU.mult).then_inc(s_xin, 1)
                pool.wait_ge(s_xin, 3 * tile + 3)
                waited()

            def product0(c, reuse):
                if reuse:
                    pool.wait_ge(s_turn[0], GROUPS[0] * c)
                    waited()
                x = xin[:, bass.ds(c * X_ROW, X_ROW)]
                wrapped = bass.AP(tensor=x.tensor, offset=x.offset, ap=[list(x.ap[0]), [1, SHIFTS], [1, FIELDS]])
                nc.gpsimd.tensor_tensor(
                    prods[:, 0:PAIRS].rearrange("p (s a) -> p s a", a=FIELDS),
                    x[:, 0:FIELDS].unsqueeze(1).broadcast_to([P, SHIFTS, FIELDS]), wrapped,
                    ALU.mult).then_inc(s_prod[0], 1)

            def product(layer, c, reuse):
                x = xin[:, bass.ds(c * X_ROW, FIELDS)]
                pool.wait_ge(s_h[layer - 1], c + 1)
                waited()
                for j in range(PIECES[layer]):
                    a, b = HSPLIT[j], HSPLIT[j + 1]
                    if reuse:
                        last = min(2 * j + 2, GROUPS[layer] - 1)
                        pool.wait_ge(s_turn[layer], GROUPS[layer] * (c - 1) + (last + 1))
                        waited()
                    nc.gpsimd.tensor_tensor(
                        prods[:, COL0[layer] + a * FIELDS:COL0[layer] + b * FIELDS].rearrange(
                            "p (h m) -> p h m", m=FIELDS),
                        h[layer - 1][:, a:b].unsqueeze(2).broadcast_to([P, b - a, FIELDS]),
                        x.unsqueeze(1).broadcast_to([P, b - a, FIELDS]), ALU.mult).then_inc(s_prod[layer], 1)

            def step(i):
                product(1, i, True)
                product0(i + 1, True)
                product(2, i - 1, True)

            nc.gpsimd.memset(ident[:], 0.0).then_inc(s_ident, 1)
            pool.wait_ge(s_ident, 1)
            nc.gpsimd.affine_select(out=ident[:], in_=ident[:], compare_op=ALU.not_equal, fill=1.0, base=0,
                                    pattern=[[-1, P]], channel_multiplier=1).then_inc(s_ident, 1)
            pool.wait_ge(s_ids, 4)
            copy_idx(0)
            for m in range(FIELDS):
                gather(m)
            pool.wait_ge(s_small, 32)
            scale(0)
            pool.wait_ge(s_pad, 1)
            product0(0, False)
            product(1, 0, False)
            product0(1, True)
            product(1, 1, True)
            product0(2, True)
            product(2, 0, False)
            with pool.Fori(0, TILES - 1) as k:
                copy_idx(k + 1)
                for j in range(DIM):
                    for m in range(4 * j, min(4 * j + 4, FIELDS)):
                        gather(m)
                    if j == 11:
                        scale(k + 1)
                    step(k * DIM + (2 + j))
            with pool.Fori(2 + DIM * (TILES - 1), LAST) as i:
                step(i)
            product(1, LAST, True)
            product(2, LAST - 1, True)
            product(2, LAST, True)

            def copy_dense(tile):
                x = xin[:, bass.ds(tile * (DIM * X_ROW), DIM * X_ROW)].rearrange("p (d x) -> p d x", x=X_ROW)
                nc.gpsimd.tensor_copy(dense_x.rearrange("p (d m) -> p d m", m=FIELDS),
                                      x[:, :, 0:FIELDS]).then_inc(s_dx, 1)

            copy_dense(0)
            with pool.Fori(1, TILES) as tile:
                pool.wait_ge(s_turn[FIRST], GROUPS[FIRST] * tile)
                waited()
                copy_dense(tile)

        @block.tensor
        def _(pe):
            def turn_group(n, slot, job, c, q):
                if not (isinstance(n, int) and n < RING):
                    pe.wait_ge(s_xlo, n - (RING - 1))
                if job == 0:
                    pe.wait_ge(s_prod[0], c + 1)
                elif job < 3:
                    pe.wait_ge(s_prod[job], PIECES[job] * c + (q // 2 + 1))
                elif job == FIRST:
                    pe.wait_ge(s_dx, c + 1)
                else:
                    pe.wait_ge(s_dh, c + 1)
                src = prods[:, COL0[job]:COL0[job] + P * KT[job]] if job < 3 else dense_x if job == FIRST else dense_h
                for t in group_tiles(job, q):
                    rows, at = ROWS[job][t], (t % GROUP) * P
                    mm = pe.transpose(turn[slot][0:rows, at:at + P], src[:, t * P:t * P + rows], ident[:])
                mm.then_inc(s_turn[job], 1)

            def multiply_group(n, slot, job, c, q):
                pe.wait_ge(s_xlo, n + 1)
                bank = acc[job] if job < 3 else acc[job - 3]
                if q == 0 and not is_first(c):
                    pe.wait_ge(s_acc[job], c)
                elif q == 0 and job >= 3:
                    pe.wait_ge(s_acc[job - 3], CHUNKS)
                    pe.wait_ge(s_dwlo, 2)
                for t in group_tiles(job, q):
                    rows, at = ROWS[job][t], (t % GROUP) * P
                    hi, lo = xhi[0:rows, slot, at:at + P], xlo[0:rows, slot, at:at + P]
                    end = t == len(ROWS[job]) - 1
                    if job < 3:
                        w = W[:, (KT0[job] + t) * 2 * OUTS:(KT0[job] + t + 1) * 2 * OUTS]
                        pe.matmul(bank[:, 0:2 * OUTS], hi, w, start=(t == 0), stop=end, skip_group_check=True)
                        mm = pe.matmul(bank[:, 0:OUTS], lo, w[:, 0:OUTS], start=False, stop=end,
                                       skip_group_check=True)
                    else:
                        k = t if job == FIRST else len(ROWS[FIRST]) + t
                        whi, wlo = dense_w[0:rows, k, 0, :], dense_w[0:rows, k, 1, :]
                        pe.matmul(bank[:, 0:DNN], hi, whi, start=(t == 0), stop=False)
                        pe.matmul(bank[:, 0:DNN], hi, wlo, start=False, stop=False)
                        mm = pe.matmul(bank[:, 0:DNN], lo, whi, start=False, stop=end)
                mm.then_inc(s_mm, 1)

            def run(n0, slot0, groups, ahead, fresh=False):
                if fresh:
                    for g in range(min(2, len(groups))):
                        turn_group(n0 + g, (slot0 + g) % RING, *groups[g])
                following = groups + ahead
                for g in range(len(groups)):
                    if g + 2 < len(following):
                        turn_group(n0 + (g + 2), (slot0 + g + 2) % RING, *following[g + 2])
                    multiply_group(n0 + g, (slot0 + g) % RING, *groups[g])

            pe.wait_ge(s_ident, 2)
            pe.wait_ge(s_pad, 1)
            run(0, 0, groups_of(0, 0), [], fresh=True)
            run(PRO, PRO, groups_of(1, 0) + groups_of(0, 1), [], fresh=True)
            run(first_group(1), 0, step_groups(1), step_groups(2)[:2], fresh=True)
            with pe.Fori(2, LAST) as i:
                run(first_group(i), 0, step_groups(i), step_groups(i + 1)[:2])
            run(first_group(LAST), 0, tail_groups(), dense_groups(2)[:2])
            with pe.Fori(2, TILES - 1) as i:
                run(dense_group(i), 2, dense_groups(i), dense_groups(i + 1)[:2])
            run(dense_group(TILES - 1), 2, dense_groups(TILES - 1), [])
            run(dense_group(TILES), 2, groups_of(SECOND, TILES - 1), [], fresh=True)

        @block.scalar
        def _(act):
            for s, i in enumerate(splits):
                if pieces[i][4] == "second":
                    act.wait_ge(s_wsum, s + 1)
                else:
                    act.wait_ge(s_stage[i % STAGES], 16 * (i // STAGES + 1))
                nc.scalar.activation(weight_half(i, 0), split_source(i), ACT.Copy).then_inc(s_whi, 1)

            def high(n, slot, job, c, q):
                act.wait_ge(s_turn[job], GROUPS[job] * c + (q + 1))
                if not (isinstance(n, int) and n < RING):
                    act.wait_ge(s_mm, n - (RING - 1))
                for rows, cols in group_parts(job, q):
                    op = nc.scalar.activation(xhi[0:rows, slot, cols], turn[slot][0:rows, cols], ACT.Copy)
                op.then_inc(s_xhi, 1)

            def low_copy(layer, c, n_last):
                act.wait_ge(s_mm, n_last + 1)
                if not is_first(c):
                    act.wait_ge(s_acc[layer], c)
                nc.scalar.activation(acc_lo[:, layer, :], acc[layer][:, OUTS:2 * OUTS],
                                     ACT.Copy).then_inc(s_acclo[layer], 1)

            def relu(layer, c):
                act.wait_ge(s_acc[layer], c + 1)
                if not is_first(c):
                    act.wait_ge(s_prod[layer + 1], PIECES[layer + 1] * c)
                nc.scalar.activation(h[layer][:], acc_sum[:, layer, 0:HID], ACT.Relu).then_inc(s_h[layer], 1)

            def dense_relu(tile):
                act.wait_ge(s_acc[FIRST], tile + 1)
                if not is_first(tile):
                    act.wait_ge(s_turn[SECOND], tile)
                nc.scalar.activation(dense_h, dense_sum[0], ACT.Relu).then_inc(s_dh, 1)

            def dense_split(n, src, k0):
                act.wait_ge(s_draw, 64)
                act.wait_ge(s_mm, first_group(LAST) + GROUPS[1])
                nc.scalar.activation(dense_w[:, k0:k0 + n, 0, :], src, ACT.Copy).then_inc(s_dwhi, 1)

            def run(n0, slot0, groups, then):
                for g in range(len(groups)):
                    high(n0 + g, (slot0 + g) % RING, *groups[g])
                    for what in then.get(g, ()):
                        what()

            run(0, 0, groups_of(0, 0), {1: [lambda: low_copy(0, 0, 1), lambda: relu(0, 0)]})
            n = PRO
            run(n, PRO, groups_of(1, 0) + groups_of(0, 1), {
                9: [lambda: low_copy(1, 0, n + 7), lambda: low_copy(0, 1, n + 9), lambda: relu(0, 1)]})

            def step(i, n, older=True):
                run(n, 0, step_groups(i), {
                    0: [lambda: relu(1, i - 1)],
                    1: [lambda: low_copy(2, i - 2, n - 1)] if older else [],
                    9: [lambda: low_copy(1, i, n + 7)],
                    11: [lambda: low_copy(0, i + 1, n + 9)],
                    12: [lambda: relu(0, i + 1)]})

            step(1, first_group(1), older=False)
            with act.Fori(2, LAST) as i:
                step(i, first_group(i))
            n = first_group(LAST)
            run(n, 0, tail_groups(), {
                0: [lambda: relu(1, LAST - 1)],
                1: [lambda: low_copy(2, LAST - 2, n - 1)],
                9: [lambda: low_copy(1, LAST, n + 7)],
                10: [lambda: relu(1, LAST)],
                17: [lambda: low_copy(2, LAST - 1, n + 15)],
                18: [lambda: dense_split(len(ROWS[FIRST]), raw_d0, 0)],
                20: [lambda: dense_split(len(ROWS[SECOND]), raw_d1, len(ROWS[FIRST]))],
                25: [lambda: low_copy(2, LAST, n + 23)],
                26: [lambda: dense_relu(0)]})
            with act.Fori(2, TILES - 1) as i:
                run(dense_group(i), 2, dense_groups(i), {0: [lambda: dense_relu(i - 1)]})
            run(dense_group(TILES - 1), 2, dense_groups(TILES - 1), {0: [lambda: dense_relu(TILES - 2)]})
            dense_relu(TILES - 1)
            run(dense_group(TILES), 2, groups_of(SECOND, TILES - 1), {})

        @block.vector
        def _(dve):
            dve.wait_ge(s_small, 32)
            nc.vector.tensor_copy(idf[:], idi[:]).then_inc(s_ids, 1)
            dve.wait_ge(s_ids, 1)
            nc.vector.tensor_scalar(neg[:], idf[:], 0.0, float(VOCAB), ALU.is_lt, ALU.mult).then_inc(s_ids, 1)
            dve.wait_ge(s_ids, 2)
            nc.vector.tensor_tensor(idf[:], idf[:], neg[:], ALU.add).then_inc(s_ids, 1)
            dve.wait_ge(s_ids, 3)
            nc.vector.tensor_scalar(idi[:], idf[:], 0.0, float(VOCAB - 1), ALU.max, ALU.min).then_inc(s_ids, 1)

            for s, i in enumerate(splits):
                if pieces[i][4] == "second":
                    for k in (i - 1, i):
                        dve.wait_ge(s_stage[k % STAGES], 16 * (k // STAGES + 1))
                    nc.vector.tensor_tensor(staged(i - 1), staged(i - 1), staged(i), ALU.add).then_inc(s_wsum, 1)
                dve.wait_ge(s_whi, s + 1)
                nc.vector.tensor_tensor(weight_half(i, 1), split_source(i), weight_half(i, 0).bitcast(F32),
                                        ALU.subtract).then_inc(s_wlo, 1)
            dve.wait_ge(s_wlo, len(splits))
            for layer in range(3):
                one = COL0[layer] + K_LAYER[layer]
                nc.vector.memset(prods[:, one:one + 1], 1.0)
                last = nc.vector.memset(prods[:, one + 1:COL0[layer] + KT[layer] * P], 0.0)
            last.then_inc(s_pad, 1)
            dve.wait_ge(s_fc, 32)

            def low(n, slot, job, c, q):
                dve.wait_ge(s_xhi, n + 1)
                for rows, cols in group_parts(job, q):
                    op = nc.vector.tensor_tensor(xlo[0:rows, slot, cols], turn[slot][0:rows, cols],
                                                 xhi[0:rows, slot, cols].bitcast(F32), ALU.subtract)
                op.then_inc(s_xlo, 1)

            def add(layer, c):
                dve.wait_ge(s_acclo[layer], c + 1)
                if not is_first(c):
                    dve.wait_ge(s_dot[layer], c)
                    if layer < 2:
                        dve.wait_ge(s_h[layer], c)
                nc.vector.tensor_tensor(acc_sum[:, layer, :], acc[layer][:, 0:OUTS], acc_lo[:, layer, :],
                                        ALU.add).then_inc(s_acc[layer], 1)

            def dot(layer, c):
                o, f, n = ((HID, 0, HID), (HID, HID, HID), (0, 2 * HID, OUTS))[layer]
                dve.wait_ge(s_acc[layer], c + 1)
                nc.vector.scalar_tensor_tensor(
                    out=spent[:, layer, 0:n], in0=acc_sum[:, layer, o:o + n], scalar=0.0, in1=fcw[:, f:f + n],
                    op0=ALU.max, op1=ALU.mult,
                    accum_out=part[:, bass.ds(c + layer * CHUNKS, 1)]).then_inc(s_dot[layer], 1)

            def dense_add(layer, tile):
                last = dense_group(tile) + 1 if layer == 0 else dense_group(tile + 1) + 2
                if layer == 0 and is_first(tile):
                    last = CIN_GROUPS + 1
                dve.wait_ge(s_mm, last + 1)
                if not is_first(tile):
                    if layer == 0:
                        dve.wait_ge(s_dh, tile)
                    else:
                        dve.wait_ge(s_ddot, tile)
                nc.vector.tensor_tensor(dense_sum[layer], acc[layer][:, 0:DNN],
                                        dense_bias[:, layer * DNN:(layer + 1) * DNN],
                                        ALU.add).then_inc(s_acc[FIRST + layer], 1)

            def dense_dot(tile):
                dve.wait_ge(s_acc[SECOND], tile + 1)
                nc.vector.scalar_tensor_tensor(
                    out=dense_spent, in0=dense_sum[1], scalar=0.0, in1=fcw[:, 2 * OUTS:2 * OUTS + DNN],
                    op0=ALU.max, op1=ALU.mult,
                    accum_out=dense_part[:, bass.ds(tile, 1)]).then_inc(s_ddot, 1)

            def dense_split(s, n, src, k0):
                dve.wait_ge(s_dwhi, s + 1)
                nc.vector.tensor_tensor(dense_w[:, k0:k0 + n, 1, :], src, dense_w[:, k0:k0 + n, 0, :].bitcast(F32),
                                        ALU.subtract).then_inc(s_dwlo, 1)

            def run(n0, slot0, groups, then):
                for g in range(len(groups)):
                    low(n0 + g, (slot0 + g) % RING, *groups[g])
                    for what in then.get(g, ()):
                        what()

            run(0, 0, groups_of(0, 0), {1: [lambda: add(0, 0), lambda: dot(0, 0)]})
            run(PRO, PRO, groups_of(1, 0) + groups_of(0, 1), {
                9: [lambda: add(1, 0), lambda: add(0, 1), lambda: dot(1, 0), lambda: dot(0, 1)]})

            def step(i, n, older=True):
                run(n, 0, step_groups(i), {
                    1: [lambda: add(2, i - 2)] if older else [],
                    2: [lambda: dot(2, i - 2)] if older else [],
                    9: [lambda: add(1, i)],
                    10: [lambda: dot(1, i)],
                    11: [lambda: add(0, i + 1)],
                    12: [lambda: dot(0, i + 1)]})

            step(1, first_group(1), older=False)
            with dve.Fori(2, LAST) as i:
                step(i, first_group(i))
            run(first_group(LAST), 0, tail_groups(), {
                1: [lambda: add(2, LAST - 2)],
                2: [lambda: dot(2, LAST - 2)],
                9: [lambda: add(1, LAST)],
                10: [lambda: dot(1, LAST)],
                17: [lambda: add(2, LAST - 1)],
                18: [lambda: dot(2, LAST - 1), lambda: dense_split(0, len(ROWS[FIRST]), raw_d0, 0)],
                20: [lambda: dense_split(1, len(ROWS[SECOND]), raw_d1, len(ROWS[FIRST]))],
                25: [lambda: add(2, LAST)],
                26: [lambda: dot(2, LAST), lambda: dense_add(0, 0)]})

            def dense_step(i):
                run(dense_group(i), 2, dense_groups(i), {
                    0: [lambda: dense_add(0, i - 1)],
                    1: [lambda: dense_add(1, i - 2), lambda: dense_dot(i - 2)]})

            with dve.Fori(2, TILES - 1) as i:
                dense_step(i)
            dense_step(TILES - 1)
            dense_add(0, TILES - 1)
            dense_add(1, TILES - 2)
            dense_dot(TILES - 2)
            run(dense_group(TILES), 2, groups_of(SECOND, TILES - 1), {})
            n = dense_group(TILES)
            dve.wait_ge(s_mm, n + 1)
            dve.wait_ge(s_ddot, TILES - 1)
            nc.vector.tensor_tensor(dense_sum[1], acc[1][:, 0:DNN], dense_bias[:, DNN:2 * DNN],
                                    ALU.add).then_inc(s_acc[SECOND], 1)
            dense_dot(TILES - 1)

            for layer in range(3):
                dve.wait_ge(s_dot[layer], CHUNKS)
            dve.wait_ge(s_xin, 3 * TILES)
            nc.vector.tensor_reduce(sums[:, 0:3 * TILES], part[:].rearrange("p (n d) -> p n d", d=DIM),
                                    AX_X, ALU.add).then_inc(s_fin, 1)
            nc.vector.tensor_reduce(sums[:, 3 * TILES:4 * TILES], fbias[:].rearrange("p (t m) -> p t m", m=FIELDS),
                                    AX_X, ALU.add).then_inc(s_fin, 1)
            dve.wait_ge(s_fin, 2)
            T = TILES
            nc.vector.tensor_tensor(total[:, 0:T], sums[:, 0:T], sums[:, T:2 * T], ALU.add).then_inc(s_fin, 1)
            nc.vector.tensor_tensor(total[:, T:2 * T], sums[:, 2 * T:3 * T], sums[:, 3 * T:4 * T],
                                    ALU.add).then_inc(s_fin, 1)
            dve.wait_ge(s_fin, 4)
            nc.vector.tensor_tensor(total[:, 2 * T:3 * T], total[:, 0:T], total[:, T:2 * T], ALU.add).then_inc(s_fin, 1)
            dve.wait_ge(s_fin, 5)
            dve.wait_ge(s_ddot, TILES)
            nc.vector.scalar_tensor_tensor(out=score[:], in0=total[:, 2 * T:3 * T], scalar=fcb[:, 0:1],
                                           in1=dense_part[:], op0=ALU.add, op1=ALU.add).then_inc(s_fin, 1)


def kernel(**inputs):
    import numpy as np
    import concourse.bacc as bacc
    from concourse.bass_utils import run_bass_kernel_spmd

    a = {k: np.asarray(v) for k, v in inputs.items()}

    def rows_to_tiles(rows, tiles):
        full = np.zeros((tiles * P, rows.shape[1]), np.float32)
        full[:rows.shape[0]] = rows
        return np.ascontiguousarray(full.reshape(tiles, P, -1).transpose(1, 0, 2))

    w0 = a["L0_rec_cin_W0"]
    field = np.arange(FIELDS)
    left = np.tile(field, SHIFTS)
    right = (left + np.repeat(np.arange(SHIFTS), FIELDS)) % FIELDS
    ab = np.concatenate([w0[:, left * FIELDS + right].T, a["L0_rec_cin_b0"][None]])
    ba = np.zeros((PAIRS, OUTS), np.float32)
    ba[FIELDS:] = w0[:, right[FIELDS:] * FIELDS + left[FIELDS:]].T
    w12 = [np.concatenate([a[f"L0_rec_cin_W{n}"].T, a[f"L0_rec_cin_b{n}"][None]]) for n in (1, 2)]
    d0 = a["L0_rec_dnn_W0"].reshape(DNN, FIELDS, DIM).transpose(2, 1, 0).reshape(DIM * FIELDS, DNN)
    arrays = {
        "vals": a["r_feature_vals"],
        "ids": a["r_feature_ids"],
        "table": np.concatenate([a["L0_rec_emb"], a["L0_rec_bias_emb"]], axis=1),
        "w0_ab": rows_to_tiles(ab, KT[0]),
        "w0_ba": rows_to_tiles(ba, KT[0]),
        "w1": rows_to_tiles(w12[0], KT[1]),
        "w2": rows_to_tiles(w12[1], KT[2]),
        "d0": rows_to_tiles(d0, len(ROWS[FIRST])),
        "d0_b": a["L0_rec_dnn_b0"],
        "d1": rows_to_tiles(a["L0_rec_dnn_W1"].T, len(ROWS[SECOND])),
        "d1_b": a["L0_rec_dnn_b1"],
        "fc_w": a["L0_rec_fc_W"].reshape(-1),
        "fc_b": a["L0_rec_fc_b"],
    }
    nc = bacc.Bacc("TRN2", target_bir_lowering=False, num_devices=1)
    args = [nc.dram_tensor(n, v.shape, mybir.dt.from_np(v.dtype), kind="ExternalInput").ap()
            for n, v in arrays.items()]
    args.append(nc.dram_tensor("scores", (BATCH,), F32, kind="ExternalOutput").ap())
    rec_kernel(nc, *args)
    r = run_bass_kernel_spmd(nc, [{n: np.ascontiguousarray(v) for n, v in arrays.items()}], core_ids=[0])
    return r.results[0]["scores"]
```

```python
from contextlib import ExitStack

import concourse.bass as bass
from concourse import mybir

P = 128
BATCH = 1024
FIELDS = 39
DIM = 16
VOCAB = 125000
EMB_COLS = DIM + 1
OUTS = 200
HID = 100
DNN = 400
TILES = BATCH // P
CHUNKS = TILES * DIM

SHIFTS = FIELDS // 2 + 1
PAIRS = SHIFTS * FIELDS
X_ROW = FIELDS + SHIFTS - 1
K_LAYER = [PAIRS, HID * FIELDS, HID * FIELDS]
KT = [-(-(k + 1) // P) for k in K_LAYER]
KT0 = [0, KT[0], KT[0] + KT[1]]
KT_ALL = sum(KT)
COL0 = [P * k for k in KT0]
QUARTER = 32
H_QUARTER = 22
H_PLAIN = HID - 4 * H_QUARTER
K_PLAIN = H_PLAIN * FIELDS
KT_PLAIN = -(-(K_PLAIN + 1) // P)
KT_QUARTERED = -(-(H_QUARTER * FIELDS) // QUARTER)
Q_COLS = QUARTER * KT_QUARTERED
GROUP = 4
GROUPS = [-(-k // GROUP) for k in KT]
RING = 3
PIECES = [1, 5, 5]
HSPLIT = [-(-(2 * GROUP * QUARTER * j) // FIELDS) for j in range(4)] + [H_QUARTER]
GROUPS_Q = GROUPS[1] - 1
assert KT_PLAIN == GROUP and KT_PLAIN + KT_QUARTERED == KT[1] == KT[2]

DENSE_K = [FIELDS * DIM, DNN]
ROWS = [[P] * k for k in KT] + [[min(P, k - t) for t in range(0, k, P)] for k in DENSE_K]
GROUPS += [-(-len(ROWS[job]) // GROUP) for job in (3, 4)]
FIRST, SECOND = 3, 4
DKT = len(ROWS[FIRST]) + len(ROWS[SECOND])

STAGE = 1000
STAGES = 8

F32 = mybir.dt.float32
F32R = mybir.dt.float32r
I32 = mybir.dt.int32
ALU = mybir.AluOpType
ACT = mybir.ActivationFunctionType
AX_X = mybir.AxisListType.X

PRO = GROUPS[0]
STEP = sum(GROUPS[0:3])
LAST = CHUNKS - 1
DENSE_STEP = GROUPS[FIRST] + GROUPS[SECOND]
CIN_GROUPS = STEP * CHUNKS


def first_group(i):
    return PRO + GROUPS[1] + GROUPS[0] + STEP * (i - 1)


def dense_group(i):
    return CIN_GROUPS + GROUPS[FIRST] + DENSE_STEP * (i - 1)


def groups_of(job, c):
    return [(job, c, q) for q in range(GROUPS[job])]


def step_groups(i):
    return groups_of(0, i + 1) + groups_of(1, i) + groups_of(2, i - 1)


def dense_groups(i):
    return groups_of(FIRST, i) + groups_of(SECOND, i - 1)


def group_tiles(job, q):
    return range(GROUP * q, min(GROUP * q + GROUP, len(ROWS[job])))


def group_parts(job, q):
    parts = []
    for t in group_tiles(job, q):
        at = (t % GROUP) * P
        if parts and parts[-1][0] == ROWS[job][t]:
            parts[-1] = (parts[-1][0], slice(parts[-1][1].start, at + P))
        else:
            parts.append((ROWS[job][t], slice(at, at + P)))
    return parts


def quartered(job, q):
    return job in (1, 2) and q > 0


def start_groups():
    return groups_of(0, 0) + groups_of(0, 1) + groups_of(1, 0)


def is_first(c):
    return isinstance(c, int) and c == 0


def tail_groups():
    return groups_of(1, LAST) + groups_of(2, LAST - 1) + groups_of(2, LAST) + groups_of(FIRST, 0) + dense_groups(1)


def rec_kernel(nc, x_store, vals, ids, table, w0_ab, w0_ba, w1, w2, d0, d0_b, d1, d1_b, fc_w, fc_b, out):
    with ExitStack() as ctx:
        def sb(name, shape, dt):
            return ctx.enter_context(nc.sbuf_tensor(name, shape, dt))

        def sem(name):
            return ctx.enter_context(nc.semaphore(name))

        W = sb("W", [P, KT_ALL * 2 * OUTS], F32R)
        prods = sb("prods", [P, KT_ALL * P], F32)
        xhi = sb("xhi", [P, RING, GROUP * P], F32R)
        xlo = sb("xlo", [P, RING, GROUP * P], F32R)
        xin = sb("xin", [P, 2 * DIM * X_ROW], F32)
        xq = sb("xq", [P, 2, 4, DIM * FIELDS], F32)
        raw = sb("raw", [P, FIELDS * EMB_COLS], F32)
        val = sb("val", [P, TILES * FIELDS], F32)
        idi = sb("idi", [P, TILES * FIELDS], I32)
        idf = sb("idf", [P, TILES * FIELDS], F32)
        neg = sb("neg", [P, TILES * FIELDS], F32)
        idx = sb("idx", [P, FIELDS], I32)
        fbias = sb("fbias", [P, TILES * FIELDS], F32)
        ident = sb("ident", [P, P], F32)
        fcw = sb("fcw", [P, 2 * OUTS + DNN], F32)
        fcb = sb("fcb", [P, 1], F32)
        acc_lo = sb("acc_lo", [P, 3, OUTS], F32)
        acc_sum = sb("acc_sum", [P, 3, OUTS], F32)
        h = [sb("h1", [P, HID], F32), sb("h2", [P, HID], F32)]
        hq = [sb("h1q", [P, 4, H_QUARTER], F32), sb("h2q", [P, 4, H_QUARTER], F32)]
        spent = sb("spent", [P, 3, OUTS], F32)
        part = sb("part", [P, 3 * CHUNKS], F32)
        dense_part = sb("dense_part", [P, TILES], F32)
        sums = sb("sums", [P, 4 * TILES], F32)
        total = sb("total", [P, 3 * TILES], F32)
        score = sb("score", [P, TILES], F32)

        n0, n1 = len(ROWS[FIRST]) * DNN, len(ROWS[SECOND]) * DNN
        raw_d0 = prods[:, 0:n0].rearrange("p (k o) -> p k o", o=DNN)
        raw_d1 = prods[:, n0:n0 + n1].rearrange("p (k o) -> p k o", o=DNN)
        dense_bias = prods[:, n0 + n1:n0 + n1 + 2 * DNN]
        dense_w = W[:, 0:DKT * 2 * DNN].rearrange("p (k two o) -> p k two o", two=2, o=DNN)
        assert n0 + n1 + 2 * DNN <= COL0[2] and DKT * 2 * DNN <= KT0[2] * 2 * OUTS
        dense_x = raw[:, 0:DENSE_K[0]]
        at = COL0[2]
        dense_sum = [prods[:, at:at + DNN], prods[:, at + DNN:at + 2 * DNN]]
        dense_h = prods[:, at + 2 * DNN:at + 3 * DNN]
        dense_spent = prods[:, at + 3 * DNN:at + 4 * DNN]

        def quartered_products(layer):
            at = COL0[layer] + KT_PLAIN * P
            return prods[:, at:at + 4 * Q_COLS].rearrange("p (q c) -> p q c", q=4)

        turn = [ctx.enter_context(nc.psum_tensor(f"turn{r}", [P, GROUP * P], F32)) for r in range(RING)]
        acc = [ctx.enter_context(nc.psum_tensor(f"acc{n}", [P, 512], F32)) for n in range(3)]

        s_small = sem("small_loaded")
        s_fc = sem("fc_loaded")
        s_stage = [sem(f"staged{n}") for n in range(STAGES)]
        s_wsum = sem("w0_summed")
        s_whi = sem("weights_high")
        s_wlo = sem("weights_low")
        s_pad = sem("pads_set")
        s_ident = sem("ident_set")
        s_ids = sem("ids_step")
        s_mark = sem("pool_waited")
        s_idx = sem("idx_copied")
        s_gather = sem("rows_gathered")
        s_xin = sem("inputs_scaled")
        s_xstore = sem("inputs_stored")
        s_xq = sem("inputs_quartered")
        s_prod = [sem(f"products{n}") for n in range(3)]
        s_turn = [sem(f"turned{n}") for n in range(5)]
        s_turnq = [None, sem("turned_quartered1"), sem("turned_quartered2")]
        s_xhi = sem("x_high")
        s_xlo = sem("x_low")
        s_mm = sem("group_multiplied")
        s_acclo = [sem(f"acc_low_copied{n}") for n in range(3)]
        s_acc = [sem(f"acc_summed{n}") for n in range(5)]
        s_h = [sem("h1_ready"), sem("h2_ready")]
        s_hq = [sem("h1_quartered"), sem("h2_quartered")]
        s_dot = [sem(f"fc_dotted{n}") for n in range(3)]
        s_draw = sem("dense_raw_loaded")
        s_dwhi = sem("dense_weights_high")
        s_dwlo = sem("dense_weights_low")
        s_dx = sem("dense_x_copied")
        s_dh = sem("dense_hidden")
        s_ddot = sem("dense_dotted")
        s_fin = sem("final_step")
        s_out = sem("output_stored")

        block = ctx.enter_context(nc.Block())

        per = STAGE // OUTS
        pieces = []
        for layer, src in ((0, w0_ab), (1, w1), (2, w2)):
            for t in range(0, KT[layer], per):
                n = min(per, KT[layer] - t)
                pieces.append((src, t, KT0[layer] + t, n, "first" if layer == 0 else "whole"))
                if layer == 0:
                    pieces.append((w0_ba, t, KT0[layer] + t, n, "second"))
        splits = [i for i, p in enumerate(pieces) if p[4] != "first"]

        def staged(i):
            return prods[:, STAGE * (i % STAGES):STAGE * (i % STAGES) + pieces[i][3] * OUTS]

        def splits_before_reuse(i):
            old = i - STAGES + (pieces[i - STAGES][4] == "first")
            return sum(1 for k in splits if k <= old)

        def split_source(i):
            return staged(i - 1 if pieces[i][4] == "second" else i).rearrange("p (k o) -> p k o", o=OUTS)

        def weight_half(i, half):
            _, _, k0, n, _ = pieces[i]
            return W[:, k0 * 2 * OUTS:(k0 + n) * 2 * OUTS].rearrange(
                "p (k two o) -> p k two o", two=2, o=OUTS)[:, :, half, :]

        @block.sync
        def _(sp):
            sp.dma_start(idi[:], ids.rearrange("(p t) m -> p (t m)", p=P)).then_inc(s_small, 16)
            sp.dma_start(val[:], vals.rearrange("(p t) m -> p (t m)", p=P)).then_inc(s_small, 16)
            for i, (src, t, k0, n, kind) in enumerate(pieces):
                if i >= STAGES:
                    sp.wait_ge(s_wlo, splits_before_reuse(i))
                sp.dma_start(staged(i).rearrange("p (k o) -> p k o", k=n),
                             src[:, t:t + n, :]).then_inc(s_stage[i % STAGES], 16)
            sp.dma_start(fcw[:], fc_w.partition_broadcast(P)).then_inc(s_fc, 16)
            sp.dma_start(fcb[:], fc_b.partition_broadcast(P)).then_inc(s_fc, 16)

            def quarter_inputs(tile, reuse):
                sp.wait_ge(s_xin, 3 * tile + 3)
                if reuse:
                    sp.wait_ge(s_prod[2], (tile - 1) * (PIECES[2] * DIM))
                sp.dma_start(x_store[bass.ds(tile * P, P), :].rearrange("p (d m) -> p d m", m=FIELDS),
                             xin[:, bass.ds((tile % 2) * (DIM * X_ROW), DIM * X_ROW)].rearrange(
                                 "p (d x) -> p d x", x=X_ROW)[:, :, 0:FIELDS]).then_inc(s_xstore, 16)
                sp.wait_ge(s_xstore, 16 * tile + 16)
                for i in range(4):
                    sp.dma_start(xq[QUARTER * i:QUARTER * (i + 1), bass.ds(tile % 2, 1), :, :].squeeze(1),
                                 x_store[bass.ds(tile * P, P), :].rearrange(
                                     "(q s) x -> s q x", q=4)).then_inc(s_xq, 16)

            quarter_inputs(0, False)
            quarter_inputs(1, False)
            with sp.Fori(2, TILES) as tile:
                quarter_inputs(tile, True)

            sp.wait_ge(s_turn[0], GROUPS[0] * CHUNKS)
            sp.wait_ge(s_turn[1], CHUNKS)
            sp.wait_ge(s_turnq[1], GROUPS_Q * CHUNKS)
            sp.dma_start(raw_d0, d0).then_inc(s_draw, 16)
            sp.dma_start(raw_d1, d1).then_inc(s_draw, 16)
            sp.dma_start(dense_bias[:, 0:DNN], d0_b.partition_broadcast(P)).then_inc(s_draw, 16)
            sp.dma_start(dense_bias[:, DNN:2 * DNN], d1_b.partition_broadcast(P)).then_inc(s_draw, 16)

            def load_dense(tile):
                sp.dma_start(dense_x, x_store[bass.ds(tile * P, P), :]).then_inc(s_dx, 16)

            load_dense(0)
            with sp.Fori(1, TILES) as tile:
                sp.wait_ge(s_turn[FIRST], GROUPS[FIRST] * tile)
                load_dense(tile)
            sp.wait_ge(s_fin, 6)
            sp.dma_start(out.rearrange("(p t) -> p t", p=P), score[:]).then_inc(s_out, 16)
            sp.wait_ge(s_out, 16)

        @block.gpsimd
        def _(pool):
            def waited():
                pool.sem_inc(s_mark, 1)

            def copy_idx(tile):
                nc.gpsimd.tensor_copy(idx[:], idi[:, bass.ds(tile * FIELDS, FIELDS)]).then_inc(s_idx, 1)
                pool.wait_ge(s_idx, tile + 1)
                waited()

            def gather(m):
                nc.gpsimd.indirect_dma_start(
                    out=raw[:, m * EMB_COLS:(m + 1) * EMB_COLS], out_offset=None, in_=table,
                    in_offset=bass.IndirectOffsetOnAxis(ap=idx[:, m:m + 1], axis=0)).then_inc(s_gather, 16)

            def scale(tile):
                pool.wait_ge(s_gather, tile * (16 * FIELDS) + 16 * FIELDS)
                waited()
                rows = raw[:].rearrange("p (m d) -> p d m", d=EMB_COLS)
                v = val[:, bass.ds(tile * FIELDS, FIELDS)]
                x = xin[:, bass.ds((tile % 2) * (DIM * X_ROW), DIM * X_ROW)].rearrange("p (d x) -> p d x", x=X_ROW)
                more = X_ROW - FIELDS
                nc.gpsimd.tensor_tensor(x[:, :, 0:FIELDS], rows[:, 0:DIM, :],
                                        v.unsqueeze(1).broadcast_to([P, DIM, FIELDS]), ALU.mult).then_inc(s_xin, 1)
                nc.gpsimd.tensor_tensor(x[:, :, FIELDS:X_ROW], rows[:, 0:DIM, 0:more],
                                        v[:, 0:more].unsqueeze(1).broadcast_to([P, DIM, more]),
                                        ALU.mult).then_inc(s_xin, 1)
                nc.gpsimd.tensor_tensor(fbias[:, bass.ds(tile * FIELDS, FIELDS)], rows[:, DIM, :], v,
                                        ALU.mult).then_inc(s_xin, 1)
                pool.wait_ge(s_xin, 3 * tile + 3)
                waited()

            def product0(c, tile, d, reuse):
                if reuse:
                    pool.wait_ge(s_turn[0], GROUPS[0] * c)
                    waited()
                x = xin[:, bass.ds((tile % 2) * (DIM * X_ROW) + d * X_ROW, X_ROW)]
                wrapped = bass.AP(tensor=x.tensor, offset=x.offset, ap=[list(x.ap[0]), [1, SHIFTS], [1, FIELDS]])
                nc.gpsimd.tensor_tensor(
                    prods[:, 0:PAIRS].rearrange("p (s a) -> p s a", a=FIELDS),
                    x[:, 0:FIELDS].unsqueeze(1).broadcast_to([P, SHIFTS, FIELDS]), wrapped,
                    ALU.mult).then_inc(s_prod[0], 1)

            def product(layer, c, tile, d, reuse):
                pool.wait_ge(s_h[layer - 1], c + 1)
                if reuse:
                    pool.wait_ge(s_turn[layer], c)
                waited()
                x = xin[:, bass.ds((tile % 2) * (DIM * X_ROW) + d * X_ROW, FIELDS)]
                nc.gpsimd.tensor_tensor(
                    prods[:, COL0[layer]:COL0[layer] + K_PLAIN].rearrange("p (h m) -> p h m", m=FIELDS),
                    h[layer - 1][:, HID - H_PLAIN:HID].unsqueeze(2).broadcast_to([P, H_PLAIN, FIELDS]),
                    x.unsqueeze(1).broadcast_to([P, H_PLAIN, FIELDS]), ALU.mult).then_inc(s_prod[layer], 1)
                pool.wait_ge(s_hq[layer - 1], 4 * c + 4)
                waited()
                out = quartered_products(layer)
                x = xq[:].rearrange("p t q x -> p (t q) x")
                x = x[:, bass.ds((tile % 2) * 4, 4), bass.ds(d * FIELDS, FIELDS)]
                for j in range(4):
                    a, b = HSPLIT[j], HSPLIT[j + 1]
                    if reuse:
                        last = min(2 * j + 3, GROUPS_Q)
                        pool.wait_ge(s_turnq[layer], GROUPS_Q * (c - 1) + last)
                        waited()
                    nc.gpsimd.tensor_tensor(
                        out[:, :, a * FIELDS:b * FIELDS].rearrange("p q (h m) -> p q h m", m=FIELDS),
                        hq[layer - 1][:, :, a:b].unsqueeze(3).broadcast_to([P, 4, b - a, FIELDS]),
                        x.unsqueeze(2).broadcast_to([P, 4, b - a, FIELDS]), ALU.mult).then_inc(s_prod[layer], 1)

            def step(k, m):
                def chunk(m):
                    return k * DIM + m, k + m // DIM, m % DIM
                product0(*chunk(m + 1), True)
                product(1, *chunk(m), True)
                product(2, *chunk(m - 1), True)

            nc.gpsimd.memset(ident[:], 0.0).then_inc(s_ident, 1)
            pool.wait_ge(s_ident, 1)
            nc.gpsimd.affine_select(out=ident[:], in_=ident[:], compare_op=ALU.not_equal, fill=1.0, base=0,
                                    pattern=[[-1, P]], channel_multiplier=1).then_inc(s_ident, 1)
            pool.wait_ge(s_ids, 4)
            copy_idx(0)
            for m in range(FIELDS):
                gather(m)
            pool.wait_ge(s_small, 32)
            scale(0)
            pool.wait_ge(s_pad, 1)
            product0(0, 0, 0, False)
            product0(1, 0, 1, True)
            pool.wait_ge(s_xq, 64)
            product(1, 0, 0, 0, False)
            product0(2, 0, 2, True)
            product(1, 1, 0, 1, True)
            product(2, 0, 0, 0, False)
            with pool.Fori(0, TILES - 1) as k:
                copy_idx(k + 1)
                for j in range(DIM):
                    for m in range(4 * j, min(4 * j + 4, FIELDS)):
                        gather(m)
                    if j == 11:
                        pool.wait_ge(s_xq, 64 * k + 64)
                        scale(k + 1)
                    if j == 14:
                        pool.wait_ge(s_xq, 64 * k + 128)
                    step(k, j + 2)
            with pool.Fori(2, DIM - 1) as d:
                t = TILES - 1
                product0(d + (t * DIM + 1), t, d + 1, True)
                product(1, d + t * DIM, t, d, True)
                product(2, d + (t * DIM - 1), t, d - 1, True)
            product(1, LAST, TILES - 1, DIM - 1, True)
            product(2, LAST - 1, TILES - 1, DIM - 2, True)
            product(2, LAST, TILES - 1, DIM - 1, True)

        @block.tensor
        def _(pe):
            def turn_group(n, slot, job, c, q):
                if not (isinstance(n, int) and n < RING):
                    pe.wait_ge(s_xlo, n - (RING - 1))
                if job == 0:
                    pe.wait_ge(s_prod[0], c + 1)
                elif job < 3:
                    pe.wait_ge(s_prod[job], PIECES[job] * c + 1)
                elif job == FIRST:
                    pe.wait_ge(s_dx, 16 * c + 16)
                else:
                    pe.wait_ge(s_dh, c + 1)
                src = prods[:, COL0[job]:COL0[job] + P * KT[job]] if job < 3 else dense_x if job == FIRST else dense_h
                for t in group_tiles(job, q):
                    rows, at = ROWS[job][t], (t % GROUP) * P
                    mm = pe.transpose(turn[slot][0:rows, at:at + P], src[:, t * P:t * P + rows], ident[:])
                mm.then_inc(s_turn[job], 1)

            def multiply_group(n, slot, job, c, q):
                pe.wait_ge(s_xlo, n + 1)
                bank = acc[job] if job < 3 else acc[job - 3]
                if q == 0 and not is_first(c):
                    pe.wait_ge(s_acc[job], c)
                elif q == 0 and job >= 3:
                    pe.wait_ge(s_acc[job - 3], CHUNKS)
                    pe.wait_ge(s_dwlo, 2)
                for t in group_tiles(job, q):
                    rows, at = ROWS[job][t], (t % GROUP) * P
                    hi, lo = xhi[0:rows, slot, at:at + P], xlo[0:rows, slot, at:at + P]
                    end = t == len(ROWS[job]) - 1
                    if job < 3:
                        w = W[:, (KT0[job] + t) * 2 * OUTS:(KT0[job] + t + 1) * 2 * OUTS]
                        pe.matmul(bank[:, 0:2 * OUTS], hi, w, start=(t == 0), stop=end, skip_group_check=True)
                        mm = pe.matmul(bank[:, 0:OUTS], lo, w[:, 0:OUTS], start=False, stop=end,
                                       skip_group_check=True)
                    else:
                        k = t if job == FIRST else len(ROWS[FIRST]) + t
                        whi, wlo = dense_w[0:rows, k, 0, :], dense_w[0:rows, k, 1, :]
                        pe.matmul(bank[:, 0:DNN], hi, whi, start=(t == 0), stop=False)
                        pe.matmul(bank[:, 0:DNN], hi, wlo, start=False, stop=False)
                        mm = pe.matmul(bank[:, 0:DNN], lo, whi, start=False, stop=end)
                mm.then_inc(s_mm, 1)

            def run(n0, slot0, groups, ahead, fresh=False):
                if fresh:
                    for g in range(min(2, len(groups))):
                        turn_group(n0 + g, (slot0 + g) % RING, *groups[g])
                following = groups + ahead
                for g in range(len(groups)):
                    if g + 2 < len(following) and not quartered(following[g + 2][0], following[g + 2][2]):
                        turn_group(n0 + (g + 2), (slot0 + g + 2) % RING, *following[g + 2])
                    multiply_group(n0 + g, (slot0 + g) % RING, *groups[g])

            pe.wait_ge(s_ident, 2)
            pe.wait_ge(s_pad, 1)
            run(0, 0, start_groups(), step_groups(1)[:2], fresh=True)
            run(first_group(1), 0, step_groups(1), step_groups(2)[:2])
            with pe.Fori(2, LAST - 1) as i:
                run(first_group(i), 0, step_groups(i), step_groups(i + 1)[:2])
            run(first_group(LAST - 1), 0, step_groups(LAST - 1), tail_groups()[:2])
            run(first_group(LAST), 0, tail_groups(), dense_groups(2)[:2])
            with pe.Fori(2, TILES - 1) as i:
                run(dense_group(i), 2, dense_groups(i), dense_groups(i + 1)[:2])
            run(dense_group(TILES - 1), 2, dense_groups(TILES - 1), [])
            run(dense_group(TILES), 2, groups_of(SECOND, TILES - 1), [], fresh=True)

        @block.scalar
        def _(act):
            for s, i in enumerate(splits):
                if pieces[i][4] == "second":
                    act.wait_ge(s_wsum, s + 1)
                else:
                    act.wait_ge(s_stage[i % STAGES], 16 * (i // STAGES + 1))
                nc.scalar.activation(weight_half(i, 0), split_source(i), ACT.Copy).then_inc(s_whi, 1)

            def high(n, slot, job, c, q):
                if quartered(job, q):
                    act.wait_ge(s_turnq[job], GROUPS_Q * c + q)
                elif job in (1, 2):
                    act.wait_ge(s_turn[job], c + 1)
                else:
                    act.wait_ge(s_turn[job], GROUPS[job] * c + (q + 1))
                if not (isinstance(n, int) and n < RING):
                    act.wait_ge(s_mm, n - (RING - 1))
                for rows, cols in group_parts(job, q):
                    op = nc.scalar.activation(xhi[0:rows, slot, cols], turn[slot][0:rows, cols], ACT.Copy)
                op.then_inc(s_xhi, 1)

            def low_copy(layer, c, n_last):
                act.wait_ge(s_mm, n_last + 1)
                if not is_first(c):
                    act.wait_ge(s_acc[layer], c)
                nc.scalar.activation(acc_lo[:, layer, :], acc[layer][:, OUTS:2 * OUTS],
                                     ACT.Copy).then_inc(s_acclo[layer], 1)

            def relu(layer, c):
                act.wait_ge(s_acc[layer], c + 1)
                if not is_first(c):
                    act.wait_ge(s_prod[layer + 1], PIECES[layer + 1] * (c - 1) + 1)
                nc.scalar.activation(h[layer][:], acc_sum[:, layer, 0:HID], ACT.Relu).then_inc(s_h[layer], 1)

            def quarter(layer, c, i):
                act.wait_ge(s_acc[layer], c + 1)
                if not is_first(c):
                    act.wait_ge(s_prod[layer + 1], PIECES[layer + 1] * c)
                for q in range(4):
                    op = nc.scalar.activation(
                        hq[layer][QUARTER * i:QUARTER * (i + 1), q, :],
                        acc_sum[QUARTER * q:QUARTER * (q + 1), layer, H_QUARTER * i:H_QUARTER * (i + 1)], ACT.Relu)
                op.then_inc(s_hq[layer], 1)

            def dense_relu(tile):
                act.wait_ge(s_acc[FIRST], tile + 1)
                if not is_first(tile):
                    act.wait_ge(s_turn[SECOND], tile)
                nc.scalar.activation(dense_h, dense_sum[0], ACT.Relu).then_inc(s_dh, 1)

            def dense_split(n, src, k0):
                act.wait_ge(s_draw, 64)
                act.wait_ge(s_mm, first_group(LAST) + GROUPS[1])
                nc.scalar.activation(dense_w[:, k0:k0 + n, 0, :], src, ACT.Copy).then_inc(s_dwhi, 1)

            def run(n0, slot0, groups, then):
                for g in range(len(groups)):
                    high(n0 + g, (slot0 + g) % RING, *groups[g])
                    for what in then.get(g, ()):
                        what()

            run(0, 0, start_groups(), {
                1: [lambda: low_copy(0, 0, 1), lambda: relu(0, 0)] + [lambda i=i: quarter(0, 0, i) for i in range(4)],
                5: [lambda: low_copy(0, 1, 3), lambda: relu(0, 1)],
                11: [lambda i=i: quarter(0, 1, i) for i in range(4)]})

            def step(i, n, second=False):
                then = {g: [] for g in range(STEP)}
                if second:
                    then[1] += [lambda: low_copy(1, i - 1, n - 1)]
                    then[2] += [lambda: relu(1, i - 1)]
                else:
                    then[1] += [lambda: low_copy(2, i - 2, n - 1)]
                for k in range(4):
                    then[k + 2 * second] += [lambda k=k: quarter(1, i - 1, k)]
                    then[k + 9] += [lambda k=k: quarter(0, i + 1, k)]
                then[3] += [lambda: low_copy(0, i + 1, n + 1)]
                then[5] += [lambda: relu(0, i + 1)]
                then[11] += [lambda: low_copy(1, i, n + 9)]
                then[13] += [lambda: relu(1, i)]
                run(n, 0, step_groups(i), then)

            step(1, first_group(1), second=True)
            with act.Fori(2, LAST - 1) as i:
                step(i, first_group(i))
            step(LAST - 1, first_group(LAST - 1))
            n = first_group(LAST)
            run(n, 0, tail_groups(), {
                0: [lambda: quarter(1, LAST - 1, 0)],
                1: [lambda: low_copy(2, LAST - 2, n - 1), lambda: quarter(1, LAST - 1, 1)],
                2: [lambda: quarter(1, LAST - 1, 2)],
                3: [lambda: quarter(1, LAST - 1, 3)],
                9: [lambda: low_copy(1, LAST, n + 7)],
                10: [lambda: relu(1, LAST)],
                11: [lambda: quarter(1, LAST, 0), lambda: quarter(1, LAST, 1)],
                12: [lambda: quarter(1, LAST, 2), lambda: quarter(1, LAST, 3)],
                17: [lambda: low_copy(2, LAST - 1, n + 15)],
                18: [lambda: dense_split(len(ROWS[FIRST]), raw_d0, 0)],
                20: [lambda: dense_split(len(ROWS[SECOND]), raw_d1, len(ROWS[FIRST]))],
                25: [lambda: low_copy(2, LAST, n + 23)],
                26: [lambda: dense_relu(0)]})
            with act.Fori(2, TILES - 1) as i:
                run(dense_group(i), 2, dense_groups(i), {0: [lambda: dense_relu(i - 1)]})
            run(dense_group(TILES - 1), 2, dense_groups(TILES - 1), {0: [lambda: dense_relu(TILES - 2)]})
            dense_relu(TILES - 1)
            run(dense_group(TILES), 2, groups_of(SECOND, TILES - 1), {})

        @block.vector
        def _(dve):
            dve.wait_ge(s_small, 32)
            nc.vector.tensor_copy(idf[:], idi[:]).then_inc(s_ids, 1)
            dve.wait_ge(s_ids, 1)
            nc.vector.tensor_scalar(neg[:], idf[:], 0.0, float(VOCAB), ALU.is_lt, ALU.mult).then_inc(s_ids, 1)
            dve.wait_ge(s_ids, 2)
            nc.vector.tensor_tensor(idf[:], idf[:], neg[:], ALU.add).then_inc(s_ids, 1)
            dve.wait_ge(s_ids, 3)
            nc.vector.tensor_scalar(idi[:], idf[:], 0.0, float(VOCAB - 1), ALU.max, ALU.min).then_inc(s_ids, 1)

            for s, i in enumerate(splits):
                if pieces[i][4] == "second":
                    for k in (i - 1, i):
                        dve.wait_ge(s_stage[k % STAGES], 16 * (k // STAGES + 1))
                    nc.vector.tensor_tensor(staged(i - 1), staged(i - 1), staged(i), ALU.add).then_inc(s_wsum, 1)
                dve.wait_ge(s_whi, s + 1)
                nc.vector.tensor_tensor(weight_half(i, 1), split_source(i), weight_half(i, 0).bitcast(F32),
                                        ALU.subtract).then_inc(s_wlo, 1)
            dve.wait_ge(s_wlo, len(splits))
            for layer in range(3):
                one = COL0[layer] + (K_PLAIN if layer else PAIRS)
                end = COL0[layer] + (KT_PLAIN if layer else KT[0]) * P
                nc.vector.memset(prods[:, one:one + 1], 1.0)
                nc.vector.memset(prods[:, one + 1:end], 0.0)
                if layer:
                    last = nc.vector.memset(quartered_products(layer)[:, :, H_QUARTER * FIELDS:Q_COLS], 0.0)
            last.then_inc(s_pad, 1)
            dve.wait_ge(s_fc, 32)

            def turn_group(n, slot, layer, c, q):
                dve.wait_ge(s_prod[layer], PIECES[layer] * c + ((q + 1) // 2 + 1))
                dve.wait_ge(s_xlo, n - (RING - 1))
                tiles = len(group_tiles(layer, q))
                first = group_tiles(layer, q)[0] - KT_PLAIN
                src = quartered_products(layer)[:, :, first * QUARTER:(first + tiles) * QUARTER]
                nc.vector.transpose(
                    turn[slot][:, 0:tiles * P].rearrange("p (t q s) -> p t q s", q=4, s=QUARTER),
                    src.rearrange("p q (t k) -> p t q k", k=QUARTER)).then_inc(s_turnq[layer], 1)

            def low(n, slot, job, c, q):
                dve.wait_ge(s_xhi, n + 1)
                for rows, cols in group_parts(job, q):
                    op = nc.vector.tensor_tensor(xlo[0:rows, slot, cols], turn[slot][0:rows, cols],
                                                 xhi[0:rows, slot, cols].bitcast(F32), ALU.subtract)
                op.then_inc(s_xlo, 1)

            def add(layer, c):
                dve.wait_ge(s_acclo[layer], c + 1)
                if not is_first(c):
                    dve.wait_ge(s_dot[layer], c)
                    if layer < 2:
                        dve.wait_ge(s_h[layer], c)
                        dve.wait_ge(s_hq[layer], 4 * c)
                nc.vector.tensor_tensor(acc_sum[:, layer, :], acc[layer][:, 0:OUTS], acc_lo[:, layer, :],
                                        ALU.add).then_inc(s_acc[layer], 1)

            def dot(layer, c):
                o, f, n = ((HID, 0, HID), (HID, HID, HID), (0, 2 * HID, OUTS))[layer]
                dve.wait_ge(s_acc[layer], c + 1)
                nc.vector.scalar_tensor_tensor(
                    out=spent[:, layer, 0:n], in0=acc_sum[:, layer, o:o + n], scalar=0.0, in1=fcw[:, f:f + n],
                    op0=ALU.max, op1=ALU.mult,
                    accum_out=part[:, bass.ds(c + layer * CHUNKS, 1)]).then_inc(s_dot[layer], 1)

            def dense_add(layer, tile):
                last = dense_group(tile) + 1 if layer == 0 else dense_group(tile + 1) + 2
                if layer == 0 and is_first(tile):
                    last = CIN_GROUPS + 1
                dve.wait_ge(s_mm, last + 1)
                if not is_first(tile):
                    if layer == 0:
                        dve.wait_ge(s_dh, tile)
                    else:
                        dve.wait_ge(s_ddot, tile)
                nc.vector.tensor_tensor(dense_sum[layer], acc[layer][:, 0:DNN],
                                        dense_bias[:, layer * DNN:(layer + 1) * DNN],
                                        ALU.add).then_inc(s_acc[FIRST + layer], 1)

            def dense_dot(tile):
                dve.wait_ge(s_acc[SECOND], tile + 1)
                nc.vector.scalar_tensor_tensor(
                    out=dense_spent, in0=dense_sum[1], scalar=0.0, in1=fcw[:, 2 * OUTS:2 * OUTS + DNN],
                    op0=ALU.max, op1=ALU.mult,
                    accum_out=dense_part[:, bass.ds(tile, 1)]).then_inc(s_ddot, 1)

            def dense_split(s, n, src, k0):
                dve.wait_ge(s_dwhi, s + 1)
                nc.vector.tensor_tensor(dense_w[:, k0:k0 + n, 1, :], src, dense_w[:, k0:k0 + n, 0, :].bitcast(F32),
                                        ALU.subtract).then_inc(s_dwlo, 1)

            def run(n0, slot0, groups, then, ahead=()):
                following = groups + list(ahead)
                for g in range(len(groups)):
                    if g + 2 < len(following) and quartered(following[g + 2][0], following[g + 2][2]):
                        turn_group(n0 + (g + 2), (slot0 + g + 2) % RING, *following[g + 2])
                    low(n0 + g, (slot0 + g) % RING, *groups[g])
                    for what in then.get(g, ()):
                        what()

            run(0, 0, start_groups(), {
                1: [lambda: add(0, 0), lambda: dot(0, 0)],
                5: [lambda: add(0, 1), lambda: dot(0, 1)]})

            def step(i, n, second=False, ahead=()):
                run(n, 0, step_groups(i), {
                    1: [(lambda: add(1, i - 1)) if second else (lambda: add(2, i - 2))],
                    2: [(lambda: dot(1, i - 1)) if second else (lambda: dot(2, i - 2))],
                    3: [lambda: add(0, i + 1)],
                    4: [lambda: dot(0, i + 1)],
                    11: [lambda: add(1, i)],
                    12: [lambda: dot(1, i)]}, ahead)

            step(1, first_group(1), second=True)
            with dve.Fori(2, LAST - 1) as i:
                step(i, first_group(i))
            step(LAST - 1, first_group(LAST - 1), ahead=tail_groups()[:2])
            run(first_group(LAST), 0, tail_groups(), {
                1: [lambda: add(2, LAST - 2)],
                2: [lambda: dot(2, LAST - 2)],
                9: [lambda: add(1, LAST)],
                10: [lambda: dot(1, LAST)],
                17: [lambda: add(2, LAST - 1)],
                18: [lambda: dot(2, LAST - 1), lambda: dense_split(0, len(ROWS[FIRST]), raw_d0, 0)],
                20: [lambda: dense_split(1, len(ROWS[SECOND]), raw_d1, len(ROWS[FIRST]))],
                25: [lambda: add(2, LAST)],
                26: [lambda: dot(2, LAST), lambda: dense_add(0, 0)]})

            def dense_step(i):
                run(dense_group(i), 2, dense_groups(i), {
                    0: [lambda: dense_add(0, i - 1)],
                    1: [lambda: dense_add(1, i - 2), lambda: dense_dot(i - 2)]})

            with dve.Fori(2, TILES - 1) as i:
                dense_step(i)
            dense_step(TILES - 1)
            dense_add(0, TILES - 1)
            dense_add(1, TILES - 2)
            dense_dot(TILES - 2)
            run(dense_group(TILES), 2, groups_of(SECOND, TILES - 1), {})
            n = dense_group(TILES)
            dve.wait_ge(s_mm, n + 1)
            dve.wait_ge(s_ddot, TILES - 1)
            nc.vector.tensor_tensor(dense_sum[1], acc[1][:, 0:DNN], dense_bias[:, DNN:2 * DNN],
                                    ALU.add).then_inc(s_acc[SECOND], 1)
            dense_dot(TILES - 1)

            for layer in range(3):
                dve.wait_ge(s_dot[layer], CHUNKS)
            dve.wait_ge(s_xin, 3 * TILES)
            nc.vector.tensor_reduce(sums[:, 0:3 * TILES], part[:].rearrange("p (n d) -> p n d", d=DIM),
                                    AX_X, ALU.add).then_inc(s_fin, 1)
            nc.vector.tensor_reduce(sums[:, 3 * TILES:4 * TILES], fbias[:].rearrange("p (t m) -> p t m", m=FIELDS),
                                    AX_X, ALU.add).then_inc(s_fin, 1)
            dve.wait_ge(s_fin, 2)
            T = TILES
            nc.vector.tensor_tensor(total[:, 0:T], sums[:, 0:T], sums[:, T:2 * T], ALU.add).then_inc(s_fin, 1)
            nc.vector.tensor_tensor(total[:, T:2 * T], sums[:, 2 * T:3 * T], sums[:, 3 * T:4 * T],
                                    ALU.add).then_inc(s_fin, 1)
            dve.wait_ge(s_fin, 4)
            nc.vector.tensor_tensor(total[:, 2 * T:3 * T], total[:, 0:T], total[:, T:2 * T], ALU.add).then_inc(s_fin, 1)
            dve.wait_ge(s_fin, 5)
            dve.wait_ge(s_ddot, TILES)
            nc.vector.scalar_tensor_tensor(out=score[:], in0=total[:, 2 * T:3 * T], scalar=fcb[:, 0:1],
                                           in1=dense_part[:], op0=ALU.add, op1=ALU.add).then_inc(s_fin, 1)


def kernel(**inputs):
    import numpy as np
    import concourse.bacc as bacc
    from concourse.bass_utils import run_bass_kernel_spmd

    a = {k: np.asarray(v) for k, v in inputs.items()}

    def rows_to_tiles(rows, tiles):
        full = np.zeros((tiles * P, rows.shape[1]), np.float32)
        full[:rows.shape[0]] = rows
        return np.ascontiguousarray(full.reshape(tiles, P, -1).transpose(1, 0, 2))

    w0 = a["L0_rec_cin_W0"]
    field = np.arange(FIELDS)
    left = np.tile(field, SHIFTS)
    right = (left + np.repeat(np.arange(SHIFTS), FIELDS)) % FIELDS
    ab = np.concatenate([w0[:, left * FIELDS + right].T, a["L0_rec_cin_b0"][None]])
    ba = np.zeros((PAIRS, OUTS), np.float32)
    ba[FIELDS:] = w0[:, right[FIELDS:] * FIELDS + left[FIELDS:]].T

    def quartered_rows(n):
        rows, n_q = a[f"L0_rec_cin_W{n}"].T, H_QUARTER * FIELDS
        plain = rows_to_tiles(np.concatenate([rows[4 * n_q:], a[f"L0_rec_cin_b{n}"][None]]), KT_PLAIN)
        full = np.zeros((4, Q_COLS, OUTS), np.float32)
        full[:, :n_q] = rows[:4 * n_q].reshape(4, n_q, OUTS)
        full = full.reshape(4, KT_QUARTERED, QUARTER, OUTS).transpose(0, 2, 1, 3).reshape(P, KT_QUARTERED, OUTS)
        return np.concatenate([plain, full], axis=1)

    d0 = a["L0_rec_dnn_W0"].reshape(DNN, FIELDS, DIM).transpose(2, 1, 0).reshape(DIM * FIELDS, DNN)
    arrays = {
        "vals": a["r_feature_vals"],
        "ids": a["r_feature_ids"],
        "table": np.concatenate([a["L0_rec_emb"], a["L0_rec_bias_emb"]], axis=1),
        "w0_ab": rows_to_tiles(ab, KT[0]),
        "w0_ba": rows_to_tiles(ba, KT[0]),
        "w1": quartered_rows(1),
        "w2": quartered_rows(2),
        "d0": rows_to_tiles(d0, len(ROWS[FIRST])),
        "d0_b": a["L0_rec_dnn_b0"],
        "d1": rows_to_tiles(a["L0_rec_dnn_W1"].T, len(ROWS[SECOND])),
        "d1_b": a["L0_rec_dnn_b1"],
        "fc_w": a["L0_rec_fc_W"].reshape(-1),
        "fc_b": a["L0_rec_fc_b"],
    }
    nc = bacc.Bacc("TRN2", target_bir_lowering=False, num_devices=1)
    args = [nc.dram_tensor(n, v.shape, mybir.dt.from_np(v.dtype), kind="ExternalInput").ap()
            for n, v in arrays.items()]
    args.append(nc.dram_tensor("scores", (BATCH,), F32, kind="ExternalOutput").ap())
    x_store = nc.dram_tensor("x_store", (BATCH, DIM * FIELDS), F32, kind="Internal").ap()
    rec_kernel(nc, x_store, *args)
    r = run_bass_kernel_spmd(nc, [{n: np.ascontiguousarray(v) for n, v in arrays.items()}], core_ids=[0])
    return r.results[0]["scores"]
```

```python
from contextlib import ExitStack

import concourse.bass as bass
from concourse import mybir

P = 128
BATCH = 1024
FIELDS = 39
DIM = 16
VOCAB = 125000
EMB_COLS = DIM + 1
OUTS = 200
HID = 100
DNN = 400
TILES = BATCH // P
CHUNKS = TILES * DIM

SHIFTS = FIELDS // 2 + 1
PAIRS = SHIFTS * FIELDS
X_ROW = FIELDS + SHIFTS - 1
K_LAYER = [PAIRS, HID * FIELDS, HID * FIELDS]
KT = [-(-(k + 1) // P) for k in K_LAYER]
KT_ALL = sum(KT)
COL0 = [P * sum(KT[:n]) for n in range(3)]
QUARTER = 32
H_QUARTER = HID // 4
Q_COLS = QUARTER * KT[1]
GROUP = 4
GROUPS = [-(-k // GROUP) for k in KT]
RING = 4
PIECES = [1, 4, 4]
HSPLIT = [-(-(2 * GROUP * QUARTER * j) // FIELDS) for j in range(4)] + [H_QUARTER]
WHOLE = [None, 6, 3]
assert 4 * Q_COLS == P * KT[1] == P * KT[2] and H_QUARTER * FIELDS < Q_COLS

DENSE_K = [FIELDS * DIM, DNN]
ROWS = [[P] * k for k in KT] + [[min(P, k - t) for t in range(0, k, P)] for k in DENSE_K]
SIZE = [GROUP, GROUP, GROUP, 2, GROUP]
GROUPS += [-(-len(ROWS[job]) // SIZE[job]) for job in (3, 4)]
FIRST, SECOND = 3, 4
DKT = len(ROWS[FIRST]) + len(ROWS[SECOND])

STAGE = 1000
STAGES = 8

F32 = mybir.dt.float32
F32R = mybir.dt.float32r
I32 = mybir.dt.int32
ALU = mybir.AluOpType
ACT = mybir.ActivationFunctionType
AX_X = mybir.AxisListType.X

SPLIT_GROUPS = [GROUPS[0], GROUPS[1] - 1, GROUPS[2] - 1]
STEP = sum(SPLIT_GROUPS)
LAST = CHUNKS - 1
DENSE_STEP = GROUPS[FIRST] + GROUPS[SECOND]
CIN_GROUPS = STEP * CHUNKS
assert STEP % RING == 0 and DENSE_STEP % RING == 0


def first_group(i):
    return 2 * SPLIT_GROUPS[0] + SPLIT_GROUPS[1] + STEP * (i - 1)


def dense_group(i):
    return CIN_GROUPS + GROUPS[FIRST] + DENSE_STEP * (i - 1)


SLOT = first_group(1) % RING
DENSE_SLOT = dense_group(1) % RING


def groups_of(job, c):
    return [(job, c, q) for q in range(GROUPS[job])]


def whole(job, q):
    return job in (1, 2) and q == WHOLE[job]


def splits_in(groups):
    return sum(1 for job, c, q in groups if not whole(job, q))


def step_groups(i):
    l0, l1 = groups_of(0, i + 1), groups_of(1, i)
    return l0[:1] + l1[:3] + l0[1:] + l1[3:] + groups_of(2, i - 1)


L0_DONE = 4
L1_DONE = 9


def dense_groups(i):
    return groups_of(FIRST, i) + groups_of(SECOND, i - 1)


def group_tiles(job, q):
    return range(SIZE[job] * q, min(SIZE[job] * (q + 1), len(ROWS[job])))


def group_parts(job, q):
    parts = []
    for t in group_tiles(job, q):
        at = (t % SIZE[job]) * P
        if parts and parts[-1][0] == ROWS[job][t]:
            parts[-1] = (parts[-1][0], slice(parts[-1][1].start, at + P))
        else:
            parts.append((ROWS[job][t], slice(at, at + P)))
    return parts


def weights_at(layer, t):
    before = sum(KT[n] - (GROUP if WHOLE[n] is not None else 0) for n in range(layer))
    skipped = WHOLE[layer] is not None and t >= GROUP * (WHOLE[layer] + 1)
    return (before + t - (GROUP if skipped else 0)) * 2 * OUTS


def start_groups():
    return groups_of(0, 0) + groups_of(0, 1) + groups_of(1, 0)


def is_first(c):
    return isinstance(c, int) and c == 0


def tail_groups():
    return groups_of(1, LAST) + groups_of(2, LAST - 1) + groups_of(2, LAST) + groups_of(FIRST, 0) + dense_groups(1)


def rec_kernel(nc, x_store, vals, ids, table, w0_ab, w0_ba, w1, w2, d0, d0_b, d1, d1_b, fc_w, fc_b, out):
    with ExitStack() as ctx:
        def sb(name, shape, dt):
            return ctx.enter_context(nc.sbuf_tensor(name, shape, dt))

        def sem(name):
            return ctx.enter_context(nc.semaphore(name))

        W = sb("W", [P, weights_at(2, KT[2])], F32R)
        w_whole = sb("w_whole", [P, 2, GROUP, OUTS], F32)
        x_whole = sb("x_whole", [P, 2, GROUP * P], F32)
        prods = sb("prods", [P, KT_ALL * P], F32)
        xhi = sb("xhi", [P, RING, GROUP * P], F32R)
        xlo = sb("xlo", [P, RING, GROUP * P], F32R)
        xin = sb("xin", [P, 2 * DIM * X_ROW], F32)
        xq = sb("xq", [P, 2, 4, DIM * FIELDS], F32)
        raw = sb("raw", [P, FIELDS * EMB_COLS], F32)
        val = sb("val", [P, TILES * FIELDS], F32)
        idi = sb("idi", [P, TILES * FIELDS], I32)
        idf = sb("idf", [P, TILES * FIELDS], F32)
        neg = sb("neg", [P, TILES * FIELDS], F32)
        idx = sb("idx", [P, FIELDS], I32)
        fbias = sb("fbias", [P, TILES * FIELDS], F32)
        ident = sb("ident", [P, P], F32)
        fcw = sb("fcw", [P, 2 * OUTS + DNN], F32)
        fcb = sb("fcb", [P, 1], F32)
        acc_lo = sb("acc_lo", [P, 3, OUTS], F32)
        acc_sum = sb("acc_sum", [P, 3, OUTS], F32)
        hq = [sb("h1q", [P, 4, H_QUARTER], F32), sb("h2q", [P, 4, H_QUARTER], F32)]
        spent = sb("spent", [P, 3, OUTS], F32)
        part = sb("part", [P, 3 * CHUNKS], F32)
        dense_part = sb("dense_part", [P, TILES], F32)
        sums = sb("sums", [P, 4 * TILES], F32)
        total = sb("total", [P, 3 * TILES], F32)
        score = sb("score", [P, TILES], F32)

        n0, n1 = len(ROWS[FIRST]) * DNN, len(ROWS[SECOND]) * DNN
        raw_d0 = prods[:, 0:n0].rearrange("p (k o) -> p k o", o=DNN)
        raw_d1 = prods[:, n0:n0 + n1].rearrange("p (k o) -> p k o", o=DNN)
        dense_bias = prods[:, n0 + n1:n0 + n1 + 2 * DNN]
        dense_w = W[:, 0:DKT * 2 * DNN].rearrange("p (k two o) -> p k two o", two=2, o=DNN)
        assert n0 + n1 + 2 * DNN <= COL0[2] and DKT * 2 * DNN <= weights_at(2, 0)
        dense_x = raw[:, 0:DENSE_K[0]]
        at = COL0[2]
        dense_sum = [prods[:, at:at + DNN], prods[:, at + DNN:at + 2 * DNN]]
        dense_h = prods[:, at + 2 * DNN:at + 3 * DNN]
        dense_spent = prods[:, at + 3 * DNN:at + 4 * DNN]

        def quartered_products(layer):
            return prods[:, COL0[layer]:COL0[layer] + 4 * Q_COLS].rearrange("p (q c) -> p q c", q=4)

        turn = [ctx.enter_context(nc.psum_tensor(f"turn{r}", [P, GROUP * P], F32)) for r in range(RING)]
        acc = [ctx.enter_context(nc.psum_tensor(f"acc{n}", [P, 512], F32)) for n in range(3)]

        s_small = sem("small_loaded")
        s_wwhole = sem("whole_weights_loaded")
        s_fc = sem("fc_loaded")
        s_stage = [sem(f"staged{n}") for n in range(STAGES)]
        s_wsum = sem("w0_summed")
        s_whi = sem("weights_high")
        s_wlo = sem("weights_low")
        s_pad = sem("pads_set")
        s_ident = sem("ident_set")
        s_ids = sem("ids_step")
        s_mark = sem("pool_waited")
        s_idx = sem("idx_copied")
        s_gather = sem("rows_gathered")
        s_xfirst = sem("first_inputs_scaled")
        s_xin = sem("inputs_scaled")
        s_xstore = sem("inputs_stored")
        s_xq = sem("inputs_quartered")
        s_prod = [sem(f"products{n}") for n in range(3)]
        s_turn = [sem(f"turned{n}") for n in range(5)]
        s_xhi = sem("x_high")
        s_xlo = sem("x_low")
        s_mm = sem("split_group_multiplied")
        s_mmw = [None, sem("whole_group1_multiplied"), sem("whole_group2_multiplied")]
        s_acclo = [sem(f"acc_low_copied{n}") for n in range(3)]
        s_acc = [sem(f"acc_summed{n}") for n in range(5)]
        s_hq = [sem("h1_quartered"), sem("h2_quartered")]
        s_dot = [sem(f"fc_dotted{n}") for n in range(3)]
        s_draw = sem("dense_raw_loaded")
        s_dwhi = sem("dense_weights_high")
        s_dwlo = sem("dense_weights_low")
        s_dx = sem("dense_x_copied")
        s_dh = sem("dense_hidden")
        s_ddot = sem("dense_dotted")
        s_fin = sem("final_step")
        s_out = sem("output_stored")

        block = ctx.enter_context(nc.Block())

        per = STAGE // OUTS
        pieces = []
        for layer, src in ((0, w0_ab), (1, w1), (2, w2)):
            for t0, t1 in ([(0, KT[0])] if layer == 0 else
                           [(0, GROUP * WHOLE[layer]), (GROUP * (WHOLE[layer] + 1), KT[layer])]):
                for t in range(t0, t1, per):
                    n = min(per, t1 - t)
                    pieces.append((src, t, weights_at(layer, t), n, "first" if layer == 0 else "whole"))
                    if layer == 0:
                        pieces.append((w0_ba, t, weights_at(layer, t), n, "second"))
        splits = [i for i, p in enumerate(pieces) if p[4] != "first"]

        def staged(i):
            return prods[:, STAGE * (i % STAGES):STAGE * (i % STAGES) + pieces[i][3] * OUTS]

        def splits_before_reuse(i):
            old = i - STAGES + (pieces[i - STAGES][4] == "first")
            return sum(1 for k in splits if k <= old)

        def split_source(i):
            return staged(i - 1 if pieces[i][4] == "second" else i).rearrange("p (k o) -> p k o", o=OUTS)

        def weight_half(i, half):
            _, _, at, n, _ = pieces[i]
            return W[:, at:at + n * 2 * OUTS].rearrange("p (k two o) -> p k two o", two=2, o=OUTS)[:, :, half, :]

        @block.sync
        def _(sp):
            sp.dma_start(idi[:], ids.rearrange("(p t) m -> p (t m)", p=P)).then_inc(s_small, 16)
            sp.dma_start(val[:], vals.rearrange("(p t) m -> p (t m)", p=P)).then_inc(s_small, 16)
            for i, (src, t, at, n, kind) in enumerate(pieces):
                if i >= STAGES:
                    sp.wait_ge(s_wlo, splits_before_reuse(i))
                sp.dma_start(staged(i).rearrange("p (k o) -> p k o", k=n),
                             src[:, t:t + n, :]).then_inc(s_stage[i % STAGES], 16)
            for n, src in ((1, w1), (2, w2)):
                sp.dma_start(w_whole[:, n - 1, :, :],
                             src[:, GROUP * WHOLE[n]:GROUP * (WHOLE[n] + 1), :]).then_inc(s_wwhole, 16)
            sp.dma_start(fcw[:], fc_w.partition_broadcast(P)).then_inc(s_fc, 16)
            sp.dma_start(fcb[:], fc_b.partition_broadcast(P)).then_inc(s_fc, 16)

            def quarter_inputs(tile, reuse):
                sp.wait_ge(s_xin, 3 * tile + 3)
                if reuse:
                    sp.wait_ge(s_prod[2], (tile - 1) * (PIECES[2] * DIM))
                sp.dma_start(x_store[bass.ds(tile * P, P), :].rearrange("p (d m) -> p d m", m=FIELDS),
                             xin[:, bass.ds((tile % 2) * (DIM * X_ROW), DIM * X_ROW)].rearrange(
                                 "p (d x) -> p d x", x=X_ROW)[:, :, 0:FIELDS]).then_inc(s_xstore, 16)
                sp.wait_ge(s_xstore, 16 * tile + 16)
                for i in range(4):
                    sp.dma_start(xq[QUARTER * i:QUARTER * (i + 1), bass.ds(tile % 2, 1), :, :].squeeze(1),
                                 x_store[bass.ds(tile * P, P), :].rearrange(
                                     "(q s) x -> s q x", q=4)).then_inc(s_xq, 16)

            sp.wait_ge(s_xfirst, 2)
            quarter_inputs(0, False)
            quarter_inputs(1, False)
            with sp.Fori(2, TILES) as tile:
                quarter_inputs(tile, True)

            sp.wait_ge(s_turn[0], GROUPS[0] * CHUNKS)
            sp.wait_ge(s_turn[1], GROUPS[1] * CHUNKS)
            sp.dma_start(raw_d0, d0).then_inc(s_draw, 16)
            sp.dma_start(raw_d1, d1).then_inc(s_draw, 16)
            sp.dma_start(dense_bias[:, 0:DNN], d0_b.partition_broadcast(P)).then_inc(s_draw, 16)
            sp.dma_start(dense_bias[:, DNN:2 * DNN], d1_b.partition_broadcast(P)).then_inc(s_draw, 16)

            def load_dense(tile):
                sp.dma_start(dense_x, x_store[bass.ds(tile * P, P), :]).then_inc(s_dx, 16)

            sp.wait_ge(s_gather, 16 * (FIELDS * TILES + sum(
                1 for m in range(FIELDS) if m * (DIM - 1) // FIELDS < 3)))
            load_dense(0)
            with sp.Fori(1, TILES) as tile:
                sp.wait_ge(s_turn[FIRST], GROUPS[FIRST] * tile)
                load_dense(tile)
            sp.wait_ge(s_fin, 6)
            sp.dma_start(out.rearrange("(p t) -> p t", p=P), score[:]).then_inc(s_out, 16)
            sp.wait_ge(s_out, 16)

        @block.gpsimd
        def _(pool):
            def waited():
                pool.sem_inc(s_mark, 1)

            def copy_idx(tile, nth):
                nc.gpsimd.tensor_copy(idx[:], idi[:, bass.ds(tile * FIELDS, FIELDS)]).then_inc(s_idx, 1)
                pool.wait_ge(s_idx, nth)
                waited()

            def gather(m):
                nc.gpsimd.indirect_dma_start(
                    out=raw[:, m * EMB_COLS:(m + 1) * EMB_COLS], out_offset=None, in_=table,
                    in_offset=bass.IndirectOffsetOnAxis(ap=idx[:, m:m + 1], axis=0)).then_inc(s_gather, 16)

            def scale_chunks(tile, first, end, done):
                rows = raw[:].rearrange("p (m d) -> p d m", d=EMB_COLS)
                v = val[:, bass.ds(tile * FIELDS, FIELDS)]
                x = xin[:, bass.ds((tile % 2) * (DIM * X_ROW), DIM * X_ROW)].rearrange("p (d x) -> p d x", x=X_ROW)
                more, n = X_ROW - FIELDS, end - first
                nc.gpsimd.tensor_tensor(x[:, first:end, 0:FIELDS], rows[:, first:end, :],
                                        v.unsqueeze(1).broadcast_to([P, n, FIELDS]), ALU.mult).then_inc(done, 1)
                nc.gpsimd.tensor_tensor(x[:, first:end, FIELDS:X_ROW], rows[:, first:end, 0:more],
                                        v[:, 0:more].unsqueeze(1).broadcast_to([P, n, more]),
                                        ALU.mult).then_inc(done, 1)

            def scale(tile, first=0):
                pool.wait_ge(s_gather, tile * (16 * FIELDS) + 16 * FIELDS)
                waited()
                scale_chunks(tile, first, DIM, s_xin)
                rows = raw[:].rearrange("p (m d) -> p d m", d=EMB_COLS)
                nc.gpsimd.tensor_tensor(fbias[:, bass.ds(tile * FIELDS, FIELDS)], rows[:, DIM, :],
                                        val[:, bass.ds(tile * FIELDS, FIELDS)], ALU.mult).then_inc(s_xin, 1)
                pool.wait_ge(s_xin, 3 * tile + 3)
                waited()

            def product0(c, tile, d, reuse):
                if reuse:
                    pool.wait_ge(s_turn[0], GROUPS[0] * c)
                    waited()
                x = xin[:, bass.ds((tile % 2) * (DIM * X_ROW) + d * X_ROW, X_ROW)]
                wrapped = bass.AP(tensor=x.tensor, offset=x.offset, ap=[list(x.ap[0]), [1, SHIFTS], [1, FIELDS]])
                nc.gpsimd.tensor_tensor(
                    prods[:, 0:PAIRS].rearrange("p (s a) -> p s a", a=FIELDS),
                    x[:, 0:FIELDS].unsqueeze(1).broadcast_to([P, SHIFTS, FIELDS]), wrapped,
                    ALU.mult).then_inc(s_prod[0], 1)

            def product(layer, c, tile, d, reuse):
                pool.wait_ge(s_hq[layer - 1], 4 * c + 4)
                waited()
                out = quartered_products(layer)
                x = xq[:].rearrange("p t q x -> p (t q) x")
                x = x[:, bass.ds((tile % 2) * 4, 4), bass.ds(d * FIELDS, FIELDS)]
                for j in range(PIECES[layer]):
                    a, b = HSPLIT[j], HSPLIT[j + 1]
                    if reuse:
                        last = min(2 * j + 3, GROUPS[layer])
                        pool.wait_ge(s_turn[layer], GROUPS[layer] * (c - 1) + last)
                        waited()
                    nc.gpsimd.tensor_tensor(
                        out[:, :, a * FIELDS:b * FIELDS].rearrange("p q (h m) -> p q h m", m=FIELDS),
                        hq[layer - 1][:, :, a:b].unsqueeze(3).broadcast_to([P, 4, b - a, FIELDS]),
                        x.unsqueeze(2).broadcast_to([P, 4, b - a, FIELDS]), ALU.mult).then_inc(s_prod[layer], 1)

            def step(k, m):
                def chunk(m):
                    return k * DIM + m, k + m // DIM, m % DIM
                product0(*chunk(m + 1), True)
                product(1, *chunk(m), True)
                product(2, *chunk(m - 1), True)

            SCALE_AT = 12

            def gathers(j):
                for m in range(FIELDS):
                    if m * (DIM - 1) // FIELDS == (j - SCALE_AT - 1) % DIM:
                        gather(m)

            nc.gpsimd.memset(ident[:], 0.0).then_inc(s_ident, 1)
            pool.wait_ge(s_ident, 1)
            nc.gpsimd.affine_select(out=ident[:], in_=ident[:], compare_op=ALU.not_equal, fill=1.0, base=0,
                                    pattern=[[-1, P]], channel_multiplier=1).then_inc(s_ident, 1)
            pool.wait_ge(s_ids, 4)
            copy_idx(0, 1)
            for m in range(FIELDS):
                gather(m)
            pool.wait_ge(s_small, 32)
            pool.wait_ge(s_gather, 16 * FIELDS)
            scale_chunks(0, 0, 1, s_xfirst)
            pool.wait_ge(s_xfirst, 2)
            pool.wait_ge(s_pad, 1)
            product0(0, 0, 0, False)
            scale(0, first=1)
            product0(1, 0, 1, True)
            copy_idx(1, 2)
            for j in range(SCALE_AT + 1, DIM):
                gathers(j)
            pool.wait_ge(s_xq, 64)
            product(1, 0, 0, 0, False)
            product0(2, 0, 2, True)
            product(1, 1, 0, 1, True)
            product(2, 0, 0, 0, False)
            with pool.Fori(0, TILES - 1) as k:
                for j in range(DIM):
                    gathers(j)
                    if j == SCALE_AT:
                        pool.wait_ge(s_xq, 64 * k + 64)
                        scale(k + 1)
                        copy_idx((k + 2) % TILES, k + 3)
                    if j == 14:
                        pool.wait_ge(s_xq, 64 * k + 128)
                    step(k, j + 2)
            with pool.Fori(2, DIM - 1) as d:
                t = TILES - 1
                product0(d + (t * DIM + 1), t, d + 1, True)
                product(1, d + t * DIM, t, d, True)
                product(2, d + (t * DIM - 1), t, d - 1, True)
            product(1, LAST, TILES - 1, DIM - 1, True)
            product(2, LAST - 1, TILES - 1, DIM - 2, True)
            product(2, LAST, TILES - 1, DIM - 1, True)

        @block.tensor
        def _(pe):
            def turn_group(n, slot, job, c, q):
                if not (isinstance(n, int) and n < RING):
                    pe.wait_ge(s_xlo, n - (RING - 1))
                if job == 0:
                    pe.wait_ge(s_prod[0], c + 1)
                elif job == FIRST:
                    pe.wait_ge(s_dx, 16 * c + 16)
                else:
                    pe.wait_ge(s_dh, c + 1)
                src = prods if job == 0 else dense_x if job == FIRST else dense_h
                for t in group_tiles(job, q):
                    rows, at = ROWS[job][t], (t % SIZE[job]) * P
                    mm = pe.transpose(turn[slot][0:rows, at:at + P], src[:, t * P:t * P + rows], ident[:])
                mm.then_inc(s_turn[job], 1)

            def multiply_group(n, slot, job, c, q):
                if whole(job, q):
                    pe.wait_ge(s_turn[job], GROUPS[job] * c + (q + 1))
                else:
                    pe.wait_ge(s_xlo, n + 1)
                bank = acc[job] if job < 3 else acc[job - 3]
                first, last = q == 0, q == GROUPS[job] - 1
                if first and not is_first(c):
                    pe.wait_ge(s_acc[job], c)
                elif first and job >= 3:
                    pe.wait_ge(s_acc[job - 3], CHUNKS)
                    pe.wait_ge(s_dwlo, 2)
                tiles = group_tiles(job, q)
                for t in tiles:
                    start, end = first and t == tiles[0], last and t == tiles[-1]
                    rows, at = ROWS[job][t], (t % SIZE[job]) * P
                    if whole(job, q):
                        mm = pe.matmul(bank[:, 0:OUTS], x_whole[:, job - 1, at:at + P],
                                       w_whole[:, job - 1, t % GROUP, :], start=False, stop=False,
                                       skip_group_check=True)
                        continue
                    hi, lo = xhi[0:rows, slot, at:at + P], xlo[0:rows, slot, at:at + P]
                    if job < 3:
                        w = W[:, weights_at(job, t):weights_at(job, t) + 2 * OUTS]
                        pe.matmul(bank[:, 0:2 * OUTS], hi, w, start=start, stop=end, skip_group_check=True)
                        mm = pe.matmul(bank[:, 0:OUTS], lo, w[:, 0:OUTS], start=False, stop=end,
                                       skip_group_check=True)
                    else:
                        k = t if job == FIRST else len(ROWS[FIRST]) + t
                        whi, wlo = dense_w[0:rows, k, 0, :], dense_w[0:rows, k, 1, :]
                        pe.matmul(bank[:, 0:DNN], hi, whi, start=start, stop=False)
                        pe.matmul(bank[:, 0:DNN], hi, wlo, start=False, stop=False)
                        mm = pe.matmul(bank[:, 0:DNN], lo, whi, start=False, stop=end)
                mm.then_inc(s_mmw[job] if whole(job, q) else s_mm, 1)

            def run(n0, slot0, groups, ahead, fresh=False, distance=2):
                following = groups + ahead

                def turn_ahead(g):
                    if g < len(following) and following[g][0] not in (1, 2):
                        before = splits_in(following[:g])
                        turn_group(n0 + before, (slot0 + before) % RING, *following[g])

                if fresh:
                    for g in range(2):
                        turn_ahead(g)
                for g in range(len(groups)):
                    turn_ahead(g + distance)
                    before = splits_in(groups[:g])
                    multiply_group(n0 + before, (slot0 + before) % RING, *groups[g])

            pe.wait_ge(s_ident, 2)
            pe.wait_ge(s_pad, 1)
            pe.wait_ge(s_wwhole, 32)
            run(0, 0, start_groups(), step_groups(1)[:2], fresh=True)
            run(first_group(1), SLOT, step_groups(1), step_groups(2)[:3], distance=3)
            with pe.Fori(2, LAST - 1) as i:
                run(first_group(i), SLOT, step_groups(i), step_groups(i + 1)[:3], distance=3)
            run(first_group(LAST - 1), SLOT, step_groups(LAST - 1), tail_groups()[:3], distance=3)
            run(first_group(LAST), SLOT, tail_groups(), dense_groups(2)[:3], distance=3)
            with pe.Fori(2, TILES - 1) as i:
                run(dense_group(i), DENSE_SLOT, dense_groups(i), dense_groups(i + 1)[:3], distance=3)
            run(dense_group(TILES - 1), DENSE_SLOT, dense_groups(TILES - 1), [], distance=3)
            run(dense_group(TILES), DENSE_SLOT, groups_of(SECOND, TILES - 1), [], fresh=True)

        @block.scalar
        def _(act):
            for s, i in enumerate(splits):
                if pieces[i][4] == "second":
                    act.wait_ge(s_wsum, s + 1)
                else:
                    act.wait_ge(s_stage[i % STAGES], 16 * (i // STAGES + 1))
                nc.scalar.activation(weight_half(i, 0), split_source(i), ACT.Copy).then_inc(s_whi, 1)

            def high(n, slot, job, c, q):
                act.wait_ge(s_turn[job], GROUPS[job] * c + (q + 1))
                if not (isinstance(n, int) and n < RING):
                    act.wait_ge(s_mm, n - (RING - 1))
                for rows, cols in group_parts(job, q):
                    op = nc.scalar.activation(xhi[0:rows, slot, cols], turn[slot][0:rows, cols], ACT.Copy)
                op.then_inc(s_xhi, 1)

            def low_copy(layer, c, n_last):
                act.wait_ge(s_mm, n_last + 1)
                if not is_first(c):
                    act.wait_ge(s_acc[layer], c)
                nc.scalar.activation(acc_lo[:, layer, :], acc[layer][:, OUTS:2 * OUTS],
                                     ACT.Copy).then_inc(s_acclo[layer], 1)

            def quarter(layer, c, i):
                act.wait_ge(s_acc[layer], c + 1)
                if not is_first(c):
                    act.wait_ge(s_prod[layer + 1], PIECES[layer + 1] * c)
                for q in range(4):
                    op = nc.scalar.activation(
                        hq[layer][QUARTER * i:QUARTER * (i + 1), q, :],
                        acc_sum[QUARTER * q:QUARTER * (q + 1), layer, H_QUARTER * i:H_QUARTER * (i + 1)], ACT.Relu)
                op.then_inc(s_hq[layer], 1)

            def dense_relu(tile):
                act.wait_ge(s_acc[FIRST], tile + 1)
                if not is_first(tile):
                    act.wait_ge(s_turn[SECOND], tile)
                nc.scalar.activation(dense_h, dense_sum[0], ACT.Relu).then_inc(s_dh, 1)

            def dense_split(n, src, k0):
                act.wait_ge(s_draw, 64)
                act.wait_ge(s_mm, first_group(LAST) + SPLIT_GROUPS[1])
                nc.scalar.activation(dense_w[:, k0:k0 + n, 0, :], src, ACT.Copy).then_inc(s_dwhi, 1)

            def run(n0, slot0, groups, then):
                for g in range(len(groups)):
                    if not whole(groups[g][0], groups[g][2]):
                        before = splits_in(groups[:g])
                        high(n0 + before, (slot0 + before) % RING, *groups[g])
                    for what in then.get(g, ()):
                        what()

            run(0, 0, start_groups(), {
                1: [lambda: low_copy(0, 0, 1)] + [lambda i=i: quarter(0, 0, i) for i in range(4)],
                5: [lambda: low_copy(0, 1, 3)],
                7: [lambda i=i: quarter(0, 1, i) for i in range(4)]})

            def step(i, n, second=False):
                groups = step_groups(i)
                then = {g: [] for g in range(len(groups))}
                if second:
                    then[1] += [lambda: low_copy(1, i - 1, n - 1)]
                    then[2] += [lambda k=k: quarter(1, i - 1, k) for k in range(4)]
                else:
                    then[2] += [lambda: low_copy(2, i - 2, n - 1)]
                then[L0_DONE + 3] += [lambda: low_copy(0, i + 1, n + splits_in(groups[:L0_DONE]))]
                for k in range(4):
                    then[L0_DONE + 4 + k // 1] += [lambda k=k: quarter(0, i + 1, k)]
                    then[L1_DONE + 5 + k // 1] += [lambda k=k: quarter(1, i, k)]
                then[L1_DONE + 3] += [lambda: low_copy(1, i, n + splits_in(groups[:L1_DONE]))]
                run(n, SLOT, groups, then)

            step(1, first_group(1), second=True)
            with act.Fori(2, LAST - 1) as i:
                step(i, first_group(i))
            step(LAST - 1, first_group(LAST - 1))
            n = first_group(LAST)
            tail = tail_groups()

            def last_number(g):
                return n + splits_in(tail[:g])

            run(n, SLOT, tail, {
                1: [lambda: low_copy(2, LAST - 2, n - 1)],
                9: [lambda: low_copy(1, LAST, last_number(7))],
                10: [lambda: quarter(1, LAST, 0), lambda: quarter(1, LAST, 1)],
                11: [lambda: quarter(1, LAST, 2), lambda: quarter(1, LAST, 3)],
                17: [lambda: low_copy(2, LAST - 1, last_number(15))],
                18: [lambda: dense_split(len(ROWS[FIRST]), raw_d0, 0)],
                20: [lambda: dense_split(len(ROWS[SECOND]), raw_d1, len(ROWS[FIRST]))],
                25: [lambda: low_copy(2, LAST, last_number(23))],
                28: [lambda: dense_relu(0)]})
            with act.Fori(2, TILES - 1) as i:
                run(dense_group(i), DENSE_SLOT, dense_groups(i), {0: [lambda: dense_relu(i - 1)]})
            run(dense_group(TILES - 1), DENSE_SLOT, dense_groups(TILES - 1), {0: [lambda: dense_relu(TILES - 2)]})
            dense_relu(TILES - 1)
            run(dense_group(TILES), DENSE_SLOT, groups_of(SECOND, TILES - 1), {})

        @block.vector
        def _(dve):
            dve.wait_ge(s_small, 32)
            nc.vector.tensor_copy(idf[:], idi[:]).then_inc(s_ids, 1)
            dve.wait_ge(s_ids, 1)
            nc.vector.tensor_scalar(neg[:], idf[:], 0.0, float(VOCAB), ALU.is_lt, ALU.mult).then_inc(s_ids, 1)
            dve.wait_ge(s_ids, 2)
            nc.vector.tensor_tensor(idf[:], idf[:], neg[:], ALU.add).then_inc(s_ids, 1)
            dve.wait_ge(s_ids, 3)
            nc.vector.tensor_scalar(idi[:], idf[:], 0.0, float(VOCAB - 1), ALU.max, ALU.min).then_inc(s_ids, 1)

            for s, i in enumerate(splits):
                if pieces[i][4] == "second":
                    for k in (i - 1, i):
                        dve.wait_ge(s_stage[k % STAGES], 16 * (k // STAGES + 1))
                    nc.vector.tensor_tensor(staged(i - 1), staged(i - 1), staged(i), ALU.add).then_inc(s_wsum, 1)
                dve.wait_ge(s_whi, s + 1)
                nc.vector.tensor_tensor(weight_half(i, 1), split_source(i), weight_half(i, 0).bitcast(F32),
                                        ALU.subtract).then_inc(s_wlo, 1)
            dve.wait_ge(s_wlo, len(splits))
            for layer in range(3):
                if layer == 0:
                    nc.vector.memset(prods[:, PAIRS:PAIRS + 1], 1.0)
                    nc.vector.memset(prods[:, PAIRS + 1:KT[0] * P], 0.0)
                else:
                    pad, one = quartered_products(layer), H_QUARTER * FIELDS
                    nc.vector.memset(pad[:, :, one:one + 1], 1.0)
                    last = nc.vector.memset(pad[:, :, one + 1:Q_COLS], 0.0)
            last.then_inc(s_pad, 1)
            dve.wait_ge(s_fc, 32)

            def turn_group(n, slot, layer, c, q):
                dve.wait_ge(s_prod[layer], PIECES[layer] * c + (q // 2 + 1))
                tiles = len(group_tiles(layer, q))
                if whole(layer, q):
                    if not is_first(c):
                        dve.wait_ge(s_mmw[layer], c)
                    place = x_whole[:, layer - 1, 0:tiles * P]
                else:
                    dve.wait_ge(s_xlo, n - (RING - 1))
                    place = turn[slot][:, 0:tiles * P]
                at = group_tiles(layer, q)[0] * QUARTER
                src = quartered_products(layer)[:, :, at:at + tiles * QUARTER]
                nc.vector.transpose(place.rearrange("p (t q s) -> p t q s", q=4, s=QUARTER),
                                    src.rearrange("p q (t k) -> p t q k", k=QUARTER)).then_inc(s_turn[layer], 1)

            def low(n, slot, job, c, q):
                dve.wait_ge(s_xhi, n + 1)
                for rows, cols in group_parts(job, q):
                    op = nc.vector.tensor_tensor(xlo[0:rows, slot, cols], turn[slot][0:rows, cols],
                                                 xhi[0:rows, slot, cols].bitcast(F32), ALU.subtract)
                op.then_inc(s_xlo, 1)

            def add(layer, c):
                dve.wait_ge(s_acclo[layer], c + 1)
                if not is_first(c):
                    dve.wait_ge(s_dot[layer], c)
                    if layer < 2:
                        dve.wait_ge(s_hq[layer], 4 * c)
                nc.vector.tensor_tensor(acc_sum[:, layer, :], acc[layer][:, 0:OUTS], acc_lo[:, layer, :],
                                        ALU.add).then_inc(s_acc[layer], 1)

            def dot(layer, c):
                o, f, n = ((HID, 0, HID), (HID, HID, HID), (0, 2 * HID, OUTS))[layer]
                dve.wait_ge(s_acc[layer], c + 1)
                nc.vector.scalar_tensor_tensor(
                    out=spent[:, layer, 0:n], in0=acc_sum[:, layer, o:o + n], scalar=0.0, in1=fcw[:, f:f + n],
                    op0=ALU.max, op1=ALU.mult,
                    accum_out=part[:, bass.ds(c + layer * CHUNKS, 1)]).then_inc(s_dot[layer], 1)

            def dense_add(layer, tile):
                last = dense_group(tile) + 2 if layer == 0 else dense_group(tile + 1) + 3
                if layer == 0 and is_first(tile):
                    last = CIN_GROUPS + 2
                dve.wait_ge(s_mm, last + 1)
                if not is_first(tile):
                    if layer == 0:
                        dve.wait_ge(s_dh, tile)
                    else:
                        dve.wait_ge(s_ddot, tile)
                nc.vector.tensor_tensor(dense_sum[layer], acc[layer][:, 0:DNN],
                                        dense_bias[:, layer * DNN:(layer + 1) * DNN],
                                        ALU.add).then_inc(s_acc[FIRST + layer], 1)

            def dense_dot(tile):
                dve.wait_ge(s_acc[SECOND], tile + 1)
                nc.vector.scalar_tensor_tensor(
                    out=dense_spent, in0=dense_sum[1], scalar=0.0, in1=fcw[:, 2 * OUTS:2 * OUTS + DNN],
                    op0=ALU.max, op1=ALU.mult,
                    accum_out=dense_part[:, bass.ds(tile, 1)]).then_inc(s_ddot, 1)

            def dense_split(s, n, src, k0):
                dve.wait_ge(s_dwhi, s + 1)
                nc.vector.tensor_tensor(dense_w[:, k0:k0 + n, 1, :], src, dense_w[:, k0:k0 + n, 0, :].bitcast(F32),
                                        ALU.subtract).then_inc(s_dwlo, 1)

            def run(n0, slot0, groups, then, ahead=()):
                following = groups + list(ahead)
                for g in range(len(groups)):
                    if g + 2 < len(following) and following[g + 2][0] in (1, 2):
                        before = splits_in(following[:g + 2])
                        turn_group(n0 + before, (slot0 + before) % RING, *following[g + 2])
                    if not whole(groups[g][0], groups[g][2]):
                        before = splits_in(groups[:g])
                        low(n0 + before, (slot0 + before) % RING, *groups[g])
                    for what in then.get(g, ()):
                        what()

            run(0, 0, start_groups(), {
                1: [lambda: add(0, 0), lambda: dot(0, 0)],
                5: [lambda: add(0, 1), lambda: dot(0, 1)]}, step_groups(1)[:2])

            def step(i, n, second=False, last=False):
                ahead = tail_groups()[:2] if last else step_groups(i + 1)[:2]
                run(n, SLOT, step_groups(i), {
                    1 if second else 2: [(lambda: add(1, i - 1)) if second else (lambda: add(2, i - 2))],
                    2 if second else 3: [(lambda: dot(1, i - 1)) if second else (lambda: dot(2, i - 2))],
                    L0_DONE + 3: [lambda: add(0, i + 1)],
                    L0_DONE + 4: [lambda: dot(0, i + 1)],
                    L1_DONE + 3: [lambda: add(1, i)],
                    L1_DONE + 4: [lambda: dot(1, i)]}, ahead)

            step(1, first_group(1), second=True)
            with dve.Fori(2, LAST - 1) as i:
                step(i, first_group(i))
            step(LAST - 1, first_group(LAST - 1), last=True)
            run(first_group(LAST), SLOT, tail_groups(), {
                1: [lambda: add(2, LAST - 2)],
                2: [lambda: dot(2, LAST - 2)],
                9: [lambda: add(1, LAST)],
                10: [lambda: dot(1, LAST)],
                17: [lambda: add(2, LAST - 1)],
                18: [lambda: dot(2, LAST - 1), lambda: dense_split(0, len(ROWS[FIRST]), raw_d0, 0)],
                20: [lambda: dense_split(1, len(ROWS[SECOND]), raw_d1, len(ROWS[FIRST]))],
                25: [lambda: add(2, LAST)],
                26: [lambda: dot(2, LAST)],
                28: [lambda: dense_add(0, 0)]})

            def dense_step(i):
                run(dense_group(i), DENSE_SLOT, dense_groups(i), {
                    0: [lambda: dense_add(0, i - 1)],
                    1: [lambda: dense_add(1, i - 2), lambda: dense_dot(i - 2)]})

            with dve.Fori(2, TILES - 1) as i:
                dense_step(i)
            dense_step(TILES - 1)
            dense_add(0, TILES - 1)
            dense_add(1, TILES - 2)
            dense_dot(TILES - 2)
            run(dense_group(TILES), DENSE_SLOT, groups_of(SECOND, TILES - 1), {})
            n = dense_group(TILES)
            dve.wait_ge(s_mm, n + 1)
            dve.wait_ge(s_ddot, TILES - 1)
            nc.vector.tensor_tensor(dense_sum[1], acc[1][:, 0:DNN], dense_bias[:, DNN:2 * DNN],
                                    ALU.add).then_inc(s_acc[SECOND], 1)
            dense_dot(TILES - 1)

            for layer in range(3):
                dve.wait_ge(s_dot[layer], CHUNKS)
            dve.wait_ge(s_xin, 3 * TILES)
            nc.vector.tensor_reduce(sums[:, 0:3 * TILES], part[:].rearrange("p (n d) -> p n d", d=DIM),
                                    AX_X, ALU.add).then_inc(s_fin, 1)
            nc.vector.tensor_reduce(sums[:, 3 * TILES:4 * TILES], fbias[:].rearrange("p (t m) -> p t m", m=FIELDS),
                                    AX_X, ALU.add).then_inc(s_fin, 1)
            dve.wait_ge(s_fin, 2)
            T = TILES
            nc.vector.tensor_tensor(total[:, 0:T], sums[:, 0:T], sums[:, T:2 * T], ALU.add).then_inc(s_fin, 1)
            nc.vector.tensor_tensor(total[:, T:2 * T], sums[:, 2 * T:3 * T], sums[:, 3 * T:4 * T],
                                    ALU.add).then_inc(s_fin, 1)
            dve.wait_ge(s_fin, 4)
            nc.vector.tensor_tensor(total[:, 2 * T:3 * T], total[:, 0:T], total[:, T:2 * T], ALU.add).then_inc(s_fin, 1)
            dve.wait_ge(s_fin, 5)
            dve.wait_ge(s_ddot, TILES)
            nc.vector.scalar_tensor_tensor(out=score[:], in0=total[:, 2 * T:3 * T], scalar=fcb[:, 0:1],
                                           in1=dense_part[:], op0=ALU.add, op1=ALU.add).then_inc(s_fin, 1)


def kernel(**inputs):
    import numpy as np
    import concourse.bacc as bacc
    from concourse.bass_utils import run_bass_kernel_spmd

    a = {k: np.asarray(v) for k, v in inputs.items()}

    def rows_to_tiles(rows, tiles):
        full = np.zeros((tiles * P, rows.shape[1]), np.float32)
        full[:rows.shape[0]] = rows
        return np.ascontiguousarray(full.reshape(tiles, P, -1).transpose(1, 0, 2))

    w0 = a["L0_rec_cin_W0"]
    field = np.arange(FIELDS)
    left = np.tile(field, SHIFTS)
    right = (left + np.repeat(np.arange(SHIFTS), FIELDS)) % FIELDS
    ab = np.concatenate([w0[:, left * FIELDS + right].T, a["L0_rec_cin_b0"][None]])
    ba = np.zeros((PAIRS, OUTS), np.float32)
    ba[FIELDS:] = w0[:, right[FIELDS:] * FIELDS + left[FIELDS:]].T

    def quartered_rows(n):
        used = H_QUARTER * FIELDS
        full = np.zeros((4, Q_COLS, OUTS), np.float32)
        full[:, :used] = a[f"L0_rec_cin_W{n}"].T.reshape(4, used, OUTS)
        full[0, used] = a[f"L0_rec_cin_b{n}"]
        return np.ascontiguousarray(
            full.reshape(4, KT[n], QUARTER, OUTS).transpose(0, 2, 1, 3).reshape(P, KT[n], OUTS))

    d0 = a["L0_rec_dnn_W0"].reshape(DNN, FIELDS, DIM).transpose(2, 1, 0).reshape(DIM * FIELDS, DNN)
    arrays = {
        "vals": a["r_feature_vals"],
        "ids": a["r_feature_ids"],
        "table": np.concatenate([a["L0_rec_emb"], a["L0_rec_bias_emb"]], axis=1),
        "w0_ab": rows_to_tiles(ab, KT[0]),
        "w0_ba": rows_to_tiles(ba, KT[0]),
        "w1": quartered_rows(1),
        "w2": quartered_rows(2),
        "d0": rows_to_tiles(d0, len(ROWS[FIRST])),
        "d0_b": a["L0_rec_dnn_b0"],
        "d1": rows_to_tiles(a["L0_rec_dnn_W1"].T, len(ROWS[SECOND])),
        "d1_b": a["L0_rec_dnn_b1"],
        "fc_w": a["L0_rec_fc_W"].reshape(-1),
        "fc_b": a["L0_rec_fc_b"],
    }
    nc = bacc.Bacc("TRN2", target_bir_lowering=False, num_devices=1)
    args = [nc.dram_tensor(n, v.shape, mybir.dt.from_np(v.dtype), kind="ExternalInput").ap()
            for n, v in arrays.items()]
    args.append(nc.dram_tensor("scores", (BATCH,), F32, kind="ExternalOutput").ap())
    x_store = nc.dram_tensor("x_store", (BATCH, DIM * FIELDS), F32, kind="Internal").ap()
    rec_kernel(nc, x_store, *args)
    r = run_bass_kernel_spmd(nc, [{n: np.ascontiguousarray(v) for n, v in arrays.items()}], core_ids=[0])
    return r.results[0]["scores"]
```
